# Optimizing a Trainium2 kernel written in Bass

```python
import numpy as np
import jax
import jax.numpy as jnp

def _softmax(x, axis=-1):
    return jax.nn.softmax(x, axis=axis)

def _gelu(x):
    return jax.nn.gelu(x, approximate=True)

def _silu(x):
    return jax.nn.silu(x)

def _sigmoid(x):
    return jax.nn.sigmoid(x)

def _layernorm(x, axis=-1, eps=1e-05):
    m = jnp.mean(x, axis=axis, keepdims=True)
    v = jnp.var(x, axis=axis, keepdims=True)
    return (x - m) / jnp.sqrt(v + eps)

def _scatter_add(tgt, idx, src, axis=0):
    return tgt.at[idx].add(src)

def _segment_sum(src, seg, n):
    return jax.ops.segment_sum(src, seg, n)
kernel_name = 'mk_rec_standalone_d1_rec_r8_1d18ba'

def setup_inputs(seed: int=0):
    np.random.seed(seed)
    _w = jnp.asarray

    def _rec_inputs():
        import jax
        import jax.numpy as jnp
        _rk = jax.random.key(seed)
        r_X = jax.random.randint(jax.random.fold_in(_rk, 1), (2048, 39), 0, 1000, jnp.int32)
        return r_X
    r_X = _rec_inputs()

    def _L0_rec_setup():
        import jax, jax.numpy as jnp
        import numpy as np
        NUM_FIELDS = 39
        VOCAB_PER_FIELD = 1000
        EMB = 64
        HEADS = 2
        LAYERS = 3
        BATCH = 2048
        FLAT = NUM_FIELDS * EMB

        def _mhsa(x, Wq, Wk, Wv, Wr):
            B, n, D = x.shape
            dh = D // HEADS
            q = (x @ Wq).reshape(B, n, HEADS, dh)
            k = (x @ Wk).reshape(B, n, HEADS, dh)
            v = (x @ Wv).reshape(B, n, HEADS, dh)
            scores = jnp.einsum('bihd,bjhd->bhij', q, k)
            attn = jax.nn.softmax(scores, axis=-1)
            out = jnp.einsum('bhij,bjhd->bihd', attn, v).reshape(B, n, D)
            out = out + x @ Wr
            return jax.nn.relu(out)
        key = jax.random.key(seed)
        ks = jax.random.split(key, 12)
        X = jax.random.randint(ks[0], (BATCH, NUM_FIELDS), 0, VOCAB_PER_FIELD, dtype=jnp.int64 if jax.config.jax_enable_x64 else jnp.int32)
        emb_table = jax.random.normal(ks[1], (NUM_FIELDS * VOCAB_PER_FIELD, EMB), jnp.float32) * 0.05
        WQ = jax.random.normal(ks[2], (LAYERS, EMB, EMB), jnp.float32) * 0.05
        WK = jax.random.normal(ks[3], (LAYERS, EMB, EMB), jnp.float32) * 0.05
        WV = jax.random.normal(ks[4], (LAYERS, EMB, EMB), jnp.float32) * 0.05
        WR = jax.random.normal(ks[5], (LAYERS, EMB, EMB), jnp.float32) * 0.05
        W1 = jax.random.normal(ks[6], (FLAT, 512), jnp.float32) * 0.02
        b1 = jnp.zeros((512,), jnp.float32)
        W2 = jax.random.normal(ks[7], (512, 256), jnp.float32) * 0.02
        b2 = jnp.zeros((256,), jnp.float32)
        W3 = jax.random.normal(ks[8], (256, 1), jnp.float32) * 0.02
        b3 = jnp.zeros((1,), jnp.float32)
        Wlin = jax.random.normal(ks[9], (FLAT, 1), jnp.float32) * 0.02
        return {'X': X, 'emb_table': emb_table, 'WQ': WQ, 'WK': WK, 'WV': WV, 'WR': WR, 'W1': W1, 'b1': b1, 'W2': W2, 'b2': b2, 'W3': W3, 'b3': b3, 'Wlin': Wlin}
    _L0_rec_all = _L0_rec_setup()
    _L0_rec_in = {k: v for k, v in _L0_rec_all.items() if k in ('emb_table', 'WQ', 'WK', 'WV', 'WR', 'W1', 'b1', 'W2', 'b2', 'W3', 'b3', 'Wlin')}
    del _L0_rec_all
    return {'r_X': r_X, 'L0_rec_emb_table': _L0_rec_in['emb_table'], 'L0_rec_WQ': _L0_rec_in['WQ'], 'L0_rec_WK': _L0_rec_in['WK'], 'L0_rec_WV': _L0_rec_in['WV'], 'L0_rec_WR': _L0_rec_in['WR'], 'L0_rec_W1': _L0_rec_in['W1'], 'L0_rec_b1': _L0_rec_in['b1'], 'L0_rec_W2': _L0_rec_in['W2'], 'L0_rec_b2': _L0_rec_in['b2'], 'L0_rec_W3': _L0_rec_in['W3'], 'L0_rec_b3': _L0_rec_in['b3'], 'L0_rec_Wlin': _L0_rec_in['Wlin']}

def reference(r_X, L0_rec_emb_table, L0_rec_WQ, L0_rec_WK, L0_rec_WV, L0_rec_WR, L0_rec_W1, L0_rec_b1, L0_rec_W2, L0_rec_b2, L0_rec_W3, L0_rec_b3, L0_rec_Wlin):
    import jax
    import jax.numpy as jnp

    def _L0_rec_ref(X, emb_table, WQ, WK, WV, WR, W1, b1, W2, b2, W3, b3, Wlin):
        import jax, jax.numpy as jnp
        import numpy as np
        NUM_FIELDS = 39
        VOCAB_PER_FIELD = 1000
        EMB = 64
        HEADS = 2
        LAYERS = 3
        BATCH = 2048
        FLAT = NUM_FIELDS * EMB

        def _mhsa(x, Wq, Wk, Wv, Wr):
            B, n, D = x.shape
            dh = D // HEADS
            q = (x @ Wq).reshape(B, n, HEADS, dh)
            k = (x @ Wk).reshape(B, n, HEADS, dh)
            v = (x @ Wv).reshape(B, n, HEADS, dh)
            scores = jnp.einsum('bihd,bjhd->bhij', q, k)
            attn = jax.nn.softmax(scores, axis=-1)
            out = jnp.einsum('bhij,bjhd->bihd', attn, v).reshape(B, n, D)
            out = out + x @ Wr
            return jax.nn.relu(out)
        offsets = jnp.arange(NUM_FIELDS, dtype=X.dtype) * VOCAB_PER_FIELD
        embed_x = emb_table[X + offsets[None, :]]
        att = embed_x
        for i in range(LAYERS):
            att = _mhsa(att, WQ[i], WK[i], WV[i], WR[i])
        B = att.shape[0]
        att_output = jax.nn.relu(att.reshape(B, FLAT) @ Wlin)
        h = embed_x.reshape(B, FLAT)
        h = jax.nn.relu(h @ W1 + b1)
        h = jax.nn.relu(h @ W2 + b2)
        dnn_output = jax.nn.relu(h @ W3 + b3)
        return jax.nn.sigmoid(att_output + dnn_output)
    y = _L0_rec_ref(r_X, L0_rec_emb_table, L0_rec_WQ, L0_rec_WK, L0_rec_WV, L0_rec_WR, L0_rec_W1, L0_rec_b1, L0_rec_W2, L0_rec_b2, L0_rec_W3, L0_rec_b3, L0_rec_Wlin)
    return y

_drawn_inputs = setup_inputs


def setup_inputs(seed=0):
    import zlib

    import numpy as np

    out = dict(_drawn_inputs(seed))
    spreads = {'L0_rec_b1': (0.0, 0.8), 'L0_rec_b2': (0.0, 0.8)}
    factors = {'L0_rec_emb_table': 8.0,
     'L0_rec_WQ': 8.0,
     'L0_rec_WK': 8.0,
     'L0_rec_WV': 8.0,
     'L0_rec_WR': 8.0,
     'L0_rec_W1': 8.0,
     'L0_rec_W2': 8.0,
     'L0_rec_W3': 8.0,
     'L0_rec_Wlin': 8.0}
    for name, (base, spread) in spreads.items():
        noise = np.random.default_rng([zlib.crc32(name.encode()), seed]).standard_normal(out[name].shape)
        drawn = base * np.exp(spread * noise) if base else spread * noise
        out[name] = jnp.asarray(drawn.astype(out[name].dtype))
    for name, factor in factors.items():
        out[name] = (out[name] * factor).astype(out[name].dtype)
    return out
```

```python
from contextlib import ExitStack

import concourse.bass as bass
from concourse import mybir

F32 = mybir.dt.float32
F32R = mybir.dt.float32r
I32 = mybir.dt.int32
ALU = mybir.AluOpType
ACTF = mybir.ActivationFunctionType
AX = mybir.AxisListType


def autoint(nc, X, table, WQ, WK, WV, WR, W1, b1, W2, b2, W3, b3, Wlin, out):
    BATCH, F = X.shape
    VOCAB = table.shape[0] // F
    D = table.shape[1]
    L = WQ.shape[0]
    H = 2
    DH = D // H
    N1, N2 = W1.shape[1], W2.shape[1]
    TB = 128
    TILES = BATCH // TB
    NP = TB // 2
    UP = 4
    C = UP * F
    UL = NP // UP
    NU = L * UL
    SL = 4
    GROUPS = NU // SL
    XC = NP * F
    FC = (F + 1) // 2
    LASTW = (F - 2 * (FC - 1)) * D
    BK = 4
    NB = FC // BK
    HF = H * F
    W = 512
    KC = N1 // 128

    ctx = ExitStack()
    with ctx:
        def sb(name, shape, dt=F32):
            return ctx.enter_context(nc.sbuf_tensor(name, shape, dt))

        def bank(name):
            return ctx.enter_context(nc.psum_tensor(name, [128, W], F32))

        def sem(name):
            return ctx.enter_context(nc.semaphore(name))

        ident = sb("ident", [128, 128])
        ones = sb("ones", [128, DH])
        sel_f = sb("sel_f", [40, UP, 2, 64])
        sel = sb("sel", [40, UP * 128], F32R)
        w_in = sb("w_in", [D, 2 * L, D])
        wT = sb("wT", [D, 2 * L, D])
        w_all = sb("w_all", [128, L, 4 * 128])
        w_grp = sb("w_grp", [128, GROUPS, 4 * 128])
        w_yv = sb("w_yv", [128, 2 * 128 + D])
        w_r = sb("w_r", [128, 128])
        w1 = sb("w1", [128, FC, N1])
        w2 = sb("w2", [128, KC, N2])
        b1_b = sb("b1_b", [128, N1])
        b2_b = sb("b2_b", [128, N2])
        w3_b = sb("w3_b", [128, N2])
        b3_b = sb("b3_b", [128, 1])
        wl_in = sb("wl_in", [F, 2, D])
        wl = sb("wl", [128, F])
        idx_in = sb("idx_in", [128, TILES, F], I32)
        f_off = sb("f_off", [128, F], I32)
        idx = sb("idx", [128, TILES * F], I32)
        idx_t = sb("idx_t", [128, F], I32)
        emb = sb("emb", [128, F * D])
        embT = sb("embT", [128, FC, TB])
        xs = sb("xs", [128, (L + 1) * XC])
        x_slot = sb("x_slot", [128, SL, UP, 64])
        y_sb = sb("y_sb", [128, 2, UP, H, F])
        v_sb = sb("v_sb", [128, SL, UP, D])
        s_sb = sb("s_sb", [128, 2, UP, HF])
        p_sb = sb("p_sb", [128, 2, UP, H, F])
        mx = sb("mx", [HF, 2 * UP])
        mhl = sb("mhl", [40, HF], F32R)
        rden = sb("rden", [128, C])
        att = sb("att", [128, C])
        pre = sb("pre", [128, 2, C])
        prod = sb("prod", [128, NP, F])
        red = sb("red", [128, TILES * NP])
        h1 = sb("h1", [128, N1])
        h1T = sb("h1T", [128, KC, 128])
        h2 = sb("h2", [128, N2])
        h2w = sb("h2w", [128, N2])
        dnn = sb("dnn", [128, TILES])
        att_o = sb("att_o", [128, TILES])
        dnn_o = sb("dnn_o", [128, TILES])
        tot = sb("tot", [128, TILES])
        y_out = sb("y_out", [TILES, 128])
        Yb, Vb, Tb, Mb, Ob, Hb = (bank(n) for n in ("Yb", "Vb", "Tb", "Mb", "Ob", "Hb"))
        Sb = [bank("S0"), bank("S1")]
        TRB = [Tb, Yb, Vb]

        ld_w = sem("ld_w")
        ld_i = sem("ld_i")
        ld_d = sem("ld_d")
        pre_pool = sem("pre_pool")
        pre_dve = sem("pre_dve")
        pre_pe = sem("pre_pe")
        weights_ready = sem("weights_ready")
        idx_ready = sem("idx_ready")
        gathered = sem("gathered")
        tr_ps = sem("tr_ps")
        embT_ready = sem("embT_ready")
        l1_ps = sem("l1_ps")
        h1_ready = sem("h1_ready")
        h1T_ps = sem("h1T_ps")
        h1T_ready = sem("h1T_ready")
        l2_ps = sem("l2_ps")
        h_free = sem("h_free")
        lin_free = sem("lin_free")
        idx_copied = sem("idx_copied")
        red_done = sem("red_done")
        dchain = sem("dchain")
        pe_passed = sem("pe_passed")
        pool_passed = sem("pool_passed")
        x_copied = sem("x_copied")
        y_ps = sem("y_ps")
        v_ps = sem("v_ps")
        y_ready = sem("y_ready")
        s_ps = sem("s_ps")
        s_ready = sem("s_ready")
        t_ps = sem("t_ps")
        m_ready = sem("m_ready")
        mt_ps = sem("mt_ps")
        hi_ready = sem("hi_ready")
        mhl_ready = sem("mhl_ready")
        e_ps = sem("e_ps")
        p_ready = sem("p_ready")
        o_ps = sem("o_ps")
        rden_ready = sem("rden_ready")
        att_ready = sem("att_ready")
        pre_ready = sem("pre_ready")
        x_new = sem("x_new")
        fin_pe = sem("fin_pe")
        fin_dve = sem("fin_dve")
        fin_act = sem("fin_act")
        stored = sem("stored")

        LD_W = 16 * (2 + 2 * L + 2 * L + 2)
        LD_D = 16 * 7

        block = ctx.enter_context(nc.Block())

        def each_group(eng, tile, step, last):
            for s in range(SL):
                step(tile * NU, 0, s, 0)
            with eng.Fori(1, GROUPS) as g:
                for s in range(SL):
                    step(tile * NU + g * SL, g, s, 1)
            for s in range(SL):
                step(tile * NU, None, s, 2)
                last(s)

        def has(part, s, k):
            return (part == 0 and s - k >= 0) or part == 1 or (part == 2 and s - k < 0)

        def count(base, part, s, k):
            return base + (NU if part == 2 else 0) + s - k + 1

        @block.sync
        def _(sp):
            sp.dma_start(idx_in[:], X.rearrange("(t p) f -> p t f", p=TB)).then_inc(ld_i, 16)
            sp.dma_start(w_in[:, 0:L, :], WQ.rearrange("l d c -> d l c")).then_inc(ld_w, 16)
            sp.dma_start(w_in[:, L:2 * L, :], WK.rearrange("l d c -> d l c")).then_inc(ld_w, 16)
            sp.wait_ge(pre_pool, 1)
            for l in range(L):
                for e in range(2):
                    lo = 64 * e
                    sp.dma_start(w_all[lo:lo + D, l, 256 + lo:256 + lo + D], WR[l]).then_inc(ld_w, 16)
                    sp.dma_start(w_all[lo:lo + D, l, 384:384 + D], WV[l]).then_inc(ld_w, 16)
            for e in range(2):
                sp.dma_start(wl_in[:, e, :], Wlin.rearrange("(f d) o -> f (d o)", f=F)).then_inc(ld_w, 16)
            sp.dma_start(w1[:, 0:FC - 1, :],
                         W1[0:(FC - 1) * 128, :].rearrange("(c p) n -> p c n", p=128)).then_inc(ld_d, 16)
            sp.dma_start(w1[0:LASTW, FC - 1, :], W1[(FC - 1) * 128:, :]).then_inc(ld_d, 16)
            sp.dma_start(w2[:], W2.rearrange("(c p) n -> p c n", p=128)).then_inc(ld_d, 16)
            sp.dma_start(b1_b[:], b1[None, :].to_broadcast([128, N1])).then_inc(ld_d, 16)
            sp.dma_start(b2_b[:], b2[None, :].to_broadcast([128, N2])).then_inc(ld_d, 16)
            sp.dma_start(w3_b[:], W3.rearrange("n o -> o n").to_broadcast([128, N2])).then_inc(ld_d, 16)
            sp.dma_start(b3_b[:], b3[None, :].to_broadcast([128, 1])).then_inc(ld_d, 16)
            sp.wait_ge(fin_act, 1)
            sp.dma_start(out.rearrange("(t p) o -> t (p o)", p=128), y_out[:]).then_inc(stored, 16)
            sp.wait_ge(stored, 16)

        @block.gpsimd
        def _(pool):
            nc.gpsimd.memset(w_all[:], 0.0).then_inc(pre_pool, 1)
            nc.gpsimd.iota(f_off[:], pattern=[[VOCAB, F]], base=0, channel_multiplier=0).then_inc(pre_pool, 1)
            nc.gpsimd.memset(ident[:], 0.0).then_inc(pre_pool, 1)
            nc.gpsimd.memset(sel_f[:], 0.0).then_inc(pre_pool, 1)
            pool.wait_ge(pre_pool, 4)
            nc.gpsimd.affine_select(out=ident[:], in_=ident[:], compare_op=ALU.not_equal, fill=1.0, base=0,
                                    pattern=[[-1, 128]], channel_multiplier=1).then_inc(pre_pool, 1)
            nc.gpsimd.affine_select(out=sel_f[:, :, :, 0:F], in_=sel_f[:, :, :, 0:F], compare_op=ALU.not_equal, fill=-1.0, base=0,
                                    pattern=[[-2, UP], [-1, 2], [0, F]], channel_multiplier=1).then_inc(pre_pool, 1)
            pool.wait_ge(pre_pool, 6)
            nc.gpsimd.affine_select(out=sel_f[:, :, :, 0:F], in_=sel_f[:, :, :, 0:F], compare_op=ALU.not_equal, fill=-1.0, base=-32,
                                    pattern=[[-2, UP], [-1, 2], [0, F]], channel_multiplier=1).then_inc(pre_pool, 1)

            def gather():
                for f in range(F):
                    nc.gpsimd.indirect_dma_start(
                        out=emb[:, f * D:(f + 1) * D], out_offset=None, in_=table,
                        in_offset=bass.IndirectOffsetOnAxis(ap=idx_t[:, f:f + 1], axis=0),
                    ).then_inc(gathered, 16)

            pool.wait_ge(idx_ready, 1)
            nc.gpsimd.tensor_copy(idx_t[:], idx[:, 0:F]).then_inc(idx_copied, 1)
            pool.wait_ge(idx_copied, 1)
            gather()

            def lin(tile):
                pool.wait_ge(x_new, tile * NU + NU)
                nc.gpsimd.tensor_tensor(prod[:], xs[:, L * XC:(L + 1) * XC].rearrange("p (n f) -> p n f", f=F),
                                        wl[:, None, :].to_broadcast([128, NP, F]), ALU.mult).then_inc(lin_free, 1)

            with pool.Fori(0, TILES - 1) as tile:
                pool.wait_ge(tr_ps, (tile + 1) * NB)
                nc.gpsimd.tensor_copy(idx_t[:], idx[:, bass.ds((tile + 1) * F, F)]).then_inc(idx_copied, 1)
                pool.wait_ge(idx_copied, tile + 2)
                pool.sem_inc(pool_passed, 1)
                gather()
                lin(tile)
            lin(TILES - 1)

        @block.tensor
        def _(pe):
            pe.wait_ge(pre_pool, 5)
            pe.wait_ge(ld_w, LD_W)
            for k in range(2 * L):
                nc.tensor.transpose(Yb[0:D, k * D:(k + 1) * D], w_in[:, k, :], ident[0:D, 0:D])
            nc.tensor.transpose(Tb[0:128, 0:F], wl_in[:].rearrange("f e d -> f (e d)"),
                                ident[0:F, 0:F]).then_inc(pre_pe, 1)
            pe.wait_ge(pre_dve, 1)
            for l in range(L):
                for h in range(H):
                    for e in range(2):
                        last = nc.tensor.matmul([Vb, Sb[0]][h][64 * e:64 * e + D, l * D:(l + 1) * D],
                                                wT[DH * h:DH * (h + 1), l, :],
                                                wT[DH * h:DH * (h + 1), L + l, :], start=True, stop=True)
            last.then_inc(pre_pe, 1)

            def embed(tile):
                pe.wait_ge(gathered, (tile + 1) * (16 * F))
                for k in range(NB):
                    if k >= 3:
                        pe.wait_ge(embT_ready, tile * NB + (k - 2))
                    for c in range(BK):
                        n = k * BK + c
                        w = LASTW if n == FC - 1 else 128
                        last = nc.tensor.transpose(TRB[k % 3][0:w, c * 128:(c + 1) * 128],
                                                   emb[:, n * 128:n * 128 + w], ident[:])
                    last.then_inc(tr_ps, 1)
                pe.wait_ge(h_free, tile + 1)
                pe.wait_ge(embT_ready, (tile + 1) * NB)
                for n in range(FC):
                    w = LASTW if n == FC - 1 else 128
                    last = nc.tensor.matmul(Hb[:], embT[0:w, n, :], w1[0:w, n, :], start=(n == 0), stop=(n == FC - 1))
                last.then_inc(l1_ps, 1)

            def step(base, g, s, part):
                def cnt(k):
                    return count(base, part, s, k)

                if has(part, s, 2):
                    pe.wait_ge(m_ready, cnt(2))
                    nc.tensor.transpose(Mb[0:2 * UP, 0:HF], mx[:], ident[0:HF, 0:HF]).then_inc(mt_ps, 1)
                if has(part, s, 3):
                    pe.wait_ge(p_ready, cnt(3))
                elif has(part, s, 1):
                    pe.wait_ge(y_ready, cnt(1))
                if has(part, s, 3) or has(part, s, 1):
                    pe.sem_inc(pe_passed, 1)
                if has(part, s, 1):
                    S = Sb[(s - 1) % 2]
                    for p in range(UP):
                        for e in range(2):
                            lo = 64 * e
                            last = nc.tensor.matmul(S[lo:lo + 64, p * HF:(p + 1) * HF],
                                                    x_slot[lo:lo + D, (s - 1) % SL, p, :],
                                                    y_sb[lo:lo + D, (s - 1) % 2, p, :, :],
                                                    start=(p == 0), stop=(p == UP - 1), skip_group_check=True)
                    last.then_inc(s_ps, 1)
                if has(part, s, 0):
                    pe.wait_ge(x_copied, cnt(0))
                    pe.sem_inc(pe_passed, 1)
                    for p in range(UP):
                        for e in range(2):
                            lo = 64 * e
                            last = nc.tensor.matmul(Vb[lo:lo + 64, p * D:(p + 1) * D],
                                                    x_slot[lo:lo + D, s, p, :],
                                                    w_yv[lo:lo + D, 256:256 + D], start=True, stop=True)
                    last.then_inc(v_ps, 1)
                    for h in range(H):
                        last = nc.tensor.matmul(Yb[:, h * C:(h + 1) * C], w_yv[:, h * 128:(h + 1) * 128],
                                                x_slot[:, s, :, 0:F], start=True, stop=True)
                    last.then_inc(y_ps, 1)
                if has(part, s, 2):
                    pe.wait_ge(mhl_ready, cnt(2))
                    for p in range(UP):
                        last = nc.tensor.matmul(Sb[s % 2][:, p * HF:(p + 1) * HF], sel[:, p * 128:(p + 1) * 128],
                                                mhl[:], start=False, stop=True, skip_group_check=True)
                    last.then_inc(e_ps, 1)
                if has(part, s, 1):
                    pe.wait_ge(s_ready, cnt(1))
                    for p in range(UP):
                        last = nc.tensor.transpose(Tb[0:HF, p * 128:(p + 1) * 128], s_sb[:, (s - 1) % 2, p, :], ident[:])
                    last.then_inc(t_ps, 1)
                if has(part, s, 3):
                    if has(part, s, 4):
                        pe.wait_ge(pre_ready, cnt(4))
                    nc.tensor.matmul(Ob[:, 2 * C:3 * C], w_r[:], x_slot[:, (s - 3) % SL, :, 0:F], start=True, stop=True)
                    for kind in range(2):
                        for p in range(UP):
                            for e in range(2):
                                for h in range(H):
                                    lo, po = 64 * e, 64 * e + DH * h
                                    left = (v_sb[lo:lo + F, (s - 3) % SL, p, DH * h:DH * (h + 1)] if kind == 0
                                            else ones[lo:lo + F, :])
                                    col = kind * C + p * F
                                    last = nc.tensor.matmul(Ob[po:po + DH, col:col + F], left,
                                                            p_sb[lo:lo + F, (s - 3) % 2, p, h, :],
                                                            start=True, stop=True)
                    last.then_inc(o_ps, 1)

            def tile_body(tile):
                embed(tile)

                def last(s):
                    if s == 0:
                        pe.wait_ge(h1_ready, tile + 1)
                        for k in range(KC):
                            t = nc.tensor.transpose(Vb[:, k * 128:(k + 1) * 128], h1[:, k * 128:(k + 1) * 128], ident[:])
                        t.then_inc(h1T_ps, 1)
                    if s == 1:
                        pe.wait_ge(h1T_ready, tile + 1)
                        for k in range(KC):
                            t = nc.tensor.matmul(Hb[:, 0:N2], h1T[:, k, :], w2[:, k, :], start=(k == 0), stop=(k == KC - 1))
                        t.then_inc(l2_ps, 1)

                each_group(pe, tile, step, last)

            pe.wait_ge(weights_ready, 1)
            pe.wait_ge(ld_d, LD_D)
            with pe.Fori(0, TILES) as tile:
                tile_body(tile)
            pe.wait_ge(red_done, TILES)
            for t in range(TILES):
                for e in range(2):
                    lo = 64 * e
                    last = nc.tensor.matmul(Yb[lo:lo + NP, t:t + 1], red[lo:lo + D, t * NP:(t + 1) * NP],
                                            ones[lo:lo + D, 0:1], start=True, stop=True)
            last.then_inc(fin_pe, 1)
            pe.wait_ge(fin_dve, 2)
            nc.tensor.transpose(Vb[0:TILES, 0:128], tot[:], ident[:]).then_inc(fin_pe, 1)

        @block.scalar
        def _(act):
            def step(base, g, s, part):
                def cnt(k):
                    return count(base, part, s, k)

                if has(part, s, 1):
                    act.wait_ge(s_ps, cnt(1))
                    nc.scalar.copy(s_sb[:, (s - 1) % 2, :, :].rearrange("q p c -> q (p c)"),
                                   Sb[(s - 1) % 2][:, 0:UP * HF]).then_inc(s_ready, 1)
                if has(part, s, 0):
                    act.wait_ge(v_ps, cnt(0))
                    nc.scalar.copy(v_sb[:, s, :, :].rearrange("q p d -> q (p d)"), Vb[:, 0:UP * D])
                    act.wait_ge(y_ps, cnt(0))
                    nc.scalar.copy(y_sb[:, s % 2, :, :, :].rearrange("q p h f -> q h p f"),
                                   Yb[:, 0:H * C].rearrange("q (h p f) -> q h p f", h=H, p=UP)).then_inc(y_ready, 1)
                if has(part, s, 4):
                    act.wait_ge(pre_ready, cnt(4))
                    if part == 1:
                        at = (g * SL + (s - 4 + UL)) * C
                    else:
                        at = ((NU if part == 2 else 0) + s - 4 + UL) * C
                    nc.scalar.activation(xs[:, bass.ds(at, C)], pre[:, s % 2, :], ACTF.Relu).then_inc(x_new, 1)
                if has(part, s, 2):
                    act.wait_ge(e_ps, cnt(2))
                    nc.scalar.activation(p_sb[:, s % 2, :, :, :].rearrange("q p h f -> q (p h f)"),
                                         Sb[s % 2][:, 0:UP * HF], ACTF.Exp).then_inc(p_ready, 1)

            with act.Fori(0, TILES) as tile:
                for k in range(NB):
                    act.wait_ge(tr_ps, tile * NB + (k + 1))
                    src = TRB[k % 3]
                    if k == NB - 1:
                        n = BK - 1
                        nc.scalar.copy(embT[:, k * BK:k * BK + n, :].rearrange("q c b -> q (c b)"), src[:, 0:n * 128])
                        nc.scalar.copy(embT[0:LASTW, k * BK + n, :], src[0:LASTW, n * 128:]).then_inc(embT_ready, 1)
                    else:
                        nc.scalar.copy(embT[:, k * BK:(k + 1) * BK, :].rearrange("q c b -> q (c b)"),
                                       src[:]).then_inc(embT_ready, 1)
                act.wait_ge(lin_free, tile + 1)

                def last(s):
                    if s == 0:
                        act.wait_ge(h1T_ps, tile + 1)
                        nc.scalar.activation(h1T[:].rearrange("q k b -> q (k b)"), Vb[:], ACTF.Relu).then_inc(h1T_ready, 1)

                each_group(act, tile, step, last)
            act.wait_ge(fin_pe, 2)
            nc.scalar.activation(y_out[:], Vb[0:TILES, 0:128], ACTF.Sigmoid).then_inc(fin_act, 1)

        @block.vector
        def _(dve):
            nc.vector.memset(x_slot[:], 0.0)
            nc.vector.memset(mhl[:].bitcast(F32), 0.0)
            nc.vector.memset(ones[:], 1.0).then_inc(h_free, 1)
            dve.wait_ge(h_free, 1)
            dve.wait_ge(ld_i, 16)
            dve.wait_ge(pre_pool, 7)
            nc.vector.tensor_tensor(idx[:].rearrange("q (t f) -> q t f", f=F), idx_in[:],
                                    f_off[:, None, :].to_broadcast([128, TILES, F]), ALU.add).then_inc(idx_ready, 1)
            nc.vector.tensor_copy(sel[:], sel_f[:].rearrange("q p e j -> q (p e j)")).then_inc(lin_free, 1)
            dve.wait_ge(pre_pe, 1)
            nc.vector.tensor_copy(wl[:], Tb[:, 0:F])
            nc.vector.tensor_copy(wT[:].rearrange("q k d -> q (k d)"), Yb[0:D, 0:2 * L * D]).then_inc(pre_dve, 1)
            dve.wait_ge(pre_pe, 2)
            for e in range(2):
                lo = 64 * e
                for h in range(H):
                    last = nc.vector.tensor_copy(
                        w_all[lo:lo + D, :, h * 128 + lo:h * 128 + lo + D],
                        [Vb, Sb[0]][h][lo:lo + D, 0:L * D].rearrange("q (l d) -> q l d", l=L))
            last.then_inc(dchain, 1)
            dve.wait_ge(dchain, 1)
            for l in range(L):
                n = GROUPS // L
                last = nc.vector.tensor_copy(w_grp[:, l * n:(l + 1) * n, :],
                                             w_all[:, l:l + 1, :].to_broadcast([128, n, 512]))
            last.then_inc(weights_ready, 1)
            dve.wait_ge(weights_ready, 1)
            dve.wait_ge(ld_d, LD_D)

            def step(base, g, s, part):
                def cnt(k):
                    return count(base, part, s, k)

                if has(part, s, 4):
                    dve.wait_ge(o_ps, cnt(4))
                if part < 2:
                    if s == 0:
                        nc.vector.tensor_copy(w_yv[:, 0:256], w_grp[:, bass.ds(g, 1), 0:256].rearrange("q g c -> q (g c)"))
                        nc.vector.tensor_copy(w_yv[:, 256:256 + D],
                                              w_grp[:, bass.ds(g, 1), 384:384 + D].rearrange("q g c -> q (g c)"))
                    if s == 3:
                        nc.vector.tensor_copy(w_r[:], w_grp[:, bass.ds(g, 1), 256:384].rearrange("q g c -> q (g c)"))
                    at = (g * SL + s) * C
                    nc.vector.tensor_copy(x_slot[:, s, :, 0:F], xs[:, bass.ds(at, C)].rearrange("q (p f) -> q p f", p=UP)).then_inc(x_copied, 1)
                if has(part, s, 2):
                    dve.wait_ge(mt_ps, cnt(2))
                    nc.vector.tensor_copy(mhl[0:2 * UP, :], Mb[0:2 * UP, 0:HF]).then_inc(hi_ready, 1)
                if has(part, s, 4):
                    nc.vector.reciprocal(rden[:], Ob[:, C:2 * C]).then_inc(rden_ready, 1)
                if has(part, s, 2):
                    dve.wait_ge(hi_ready, cnt(2))
                    nc.vector.tensor_tensor(mhl[32:32 + 2 * UP, :], Mb[0:2 * UP, 0:HF],
                                            mhl[0:2 * UP, :].bitcast(F32), ALU.subtract).then_inc(mhl_ready, 1)
                if has(part, s, 4):
                    dve.wait_ge(rden_ready, cnt(4))
                    nc.vector.tensor_tensor(att[:], Ob[:, 0:C], rden[:], ALU.mult).then_inc(att_ready, 1)
                    dve.wait_ge(att_ready, cnt(4))
                    nc.vector.tensor_tensor(pre[:, s % 2, :], Ob[:, 2 * C:3 * C], att[:], ALU.add).then_inc(pre_ready, 1)
                if has(part, s, 1):
                    dve.wait_ge(t_ps, cnt(1))
                    nc.vector.tensor_reduce(mx[:], Tb[0:HF, :].rearrange("q (n j) -> q n j", j=64)[:, :, 0:F],
                                            AX.X, ALU.max).then_inc(m_ready, 1)

            with dve.Fori(0, TILES) as tile:
                for k in range(NB):
                    dve.wait_ge(embT_ready, tile * NB + (k + 1))
                    for e in range(2):
                        for odd in range(2):
                            n = BK - 1 if odd and k == NB - 1 else BK
                            src = embT[64 * odd:64 * odd + D, k * BK:k * BK + n, NP * e:NP * (e + 1)]
                            dst = xs[64 * e:64 * e + D, 0:XC].rearrange("q (p f) -> q f p", f=F)
                            f0 = 2 * BK * k + odd
                            last = nc.vector.tensor_copy(dst[:, f0:f0 + 2 * (n - 1) + 1:2, :], src)
                last.then_inc(dchain, 1)
                dve.wait_ge(dchain, tile * 3 + 2)
                dve.wait_ge(l1_ps, tile + 1)
                nc.vector.tensor_tensor(h1[:], Hb[:], b1_b[:], ALU.add).then_inc(h1_ready, 1)

                def last_steps(s):
                    if s == 1:
                        dve.wait_ge(l2_ps, tile + 1)
                        nc.vector.tensor_tensor(h2[:], Hb[:, 0:N2], b2_b[:], ALU.add).then_inc(h_free, 1)
                        dve.wait_ge(h_free, tile + 2)
                        nc.vector.scalar_tensor_tensor(out=h2w[:], in0=h2[:], scalar=0.0, in1=w3_b[:],
                                                       op0=ALU.max, op1=ALU.mult).then_inc(dchain, 1)
                        dve.wait_ge(dchain, tile * 3 + 3)
                        nc.vector.tensor_reduce(dnn[:, bass.ds(tile, 1)], h2w[:], AX.X, ALU.add).then_inc(dchain, 1)

                each_group(dve, tile, step, last_steps)
                dve.wait_ge(lin_free, tile + 2)
                nc.vector.tensor_reduce(red[:, bass.ds(tile * NP, NP)], prod[:], AX.X, ALU.add).then_inc(red_done, 1)
            dve.wait_ge(fin_pe, 1)
            nc.vector.tensor_scalar(att_o[:], Yb[:, 0:TILES], 0.0, None, ALU.max)
            nc.vector.tensor_scalar(dnn_o[:], dnn[:], b3_b[:, 0:1], 0.0, ALU.add, ALU.max).then_inc(fin_dve, 1)
            dve.wait_ge(fin_dve, 1)
            nc.vector.tensor_tensor(tot[:], att_o[:], dnn_o[:], ALU.add).then_inc(fin_dve, 1)


_INS = ["r_X", "L0_rec_emb_table", "L0_rec_WQ", "L0_rec_WK", "L0_rec_WV", "L0_rec_WR", "L0_rec_W1", "L0_rec_b1",
        "L0_rec_W2", "L0_rec_b2", "L0_rec_W3", "L0_rec_b3", "L0_rec_Wlin"]


def kernel(**inputs):
    import numpy as np
    import concourse.bacc as bacc
    from concourse.bass_utils import run_bass_kernel_spmd

    nc = bacc.Bacc("TRN2", target_bir_lowering=False, num_devices=1)
    arrays, args = {}, []
    for name in _INS:
        a = np.ascontiguousarray(inputs[name])
        arrays[name] = a
        args.append(nc.dram_tensor(name, a.shape, mybir.dt.from_np(a.dtype), kind="ExternalInput").ap())
    out = nc.dram_tensor("y", (inputs["r_X"].shape[0], 1), F32, kind="ExternalOutput").ap()
    autoint(nc, *args, out)
    r = run_bass_kernel_spmd(nc, [arrays], core_ids=[0])
    return r.results[0]["y"]
```

```python
from contextlib import ExitStack

import concourse.bass as bass
from concourse import mybir

F32 = mybir.dt.float32
F32R = mybir.dt.float32r
I32 = mybir.dt.int32
ALU = mybir.AluOpType
ACTF = mybir.ActivationFunctionType
AX = mybir.AxisListType


def autoint(nc, X, table, WQ, WK, WV, WR, W1, b1, W2, b2, W3, b3, Wlin, out):
    BATCH, F = X.shape
    VOCAB = table.shape[0] // F
    D = table.shape[1]
    L = WQ.shape[0]
    H = 2
    DH = D // H
    N1, N2 = W1.shape[1], W2.shape[1]
    TB = 128
    TILES = BATCH // TB
    NP = TB // 2
    UP = 4
    C = UP * F
    UL = NP // UP
    NU = L * UL
    SL = 4
    GROUPS = NU // SL
    XC = NP * F
    FC = (F + 1) // 2
    LASTW = (F - 2 * (FC - 1)) * D
    BK = 4
    NB = FC // BK
    HF = H * F
    KR = 64 + F
    W = 512
    KC = N1 // 128

    ctx = ExitStack()
    with ctx:
        def sb(name, shape, dt=F32):
            return ctx.enter_context(nc.sbuf_tensor(name, shape, dt))

        def bank(name):
            return ctx.enter_context(nc.psum_tensor(name, [128, W], F32))

        def sem(name):
            return ctx.enter_context(nc.semaphore(name))

        ident = sb("ident", [128, 128])
        ones = sb("ones", [128, 2, DH])
        ones_c = sb("ones_c", [128, 1])
        sel_f = sb("sel_f", [40, UP, KR])
        sel = sb("sel", [40, UP * KR], F32R)
        w_in = sb("w_in", [D, 2 * L, D])
        wT = sb("wT", [D, 2 * L, D])
        w_all = sb("w_all", [128, L, 4 * 128])
        w_grp = sb("w_grp", [128, GROUPS, 4 * 128])
        w_y = sb("w_y", [128, 2 * 128])
        w_r = sb("w_r", [128, 128])
        w1 = sb("w1", [128, FC, N1])
        w2 = sb("w2", [128, KC, N2])
        b1_b = sb("b1_b", [128, N1])
        b2_b = sb("b2_b", [128, N2])
        w3_b = sb("w3_b", [128, N2])
        b3_b = sb("b3_b", [128, 1])
        wl_in = sb("wl_in", [F, 2, D])
        wl = sb("wl", [128, F])
        idx_in = sb("idx_in", [128, TILES, F], I32)
        f_off = sb("f_off", [128, F], I32)
        idx = sb("idx", [128, TILES * F], I32)
        idx_t = sb("idx_t", [128, F], I32)
        emb = sb("emb", [128, F * D])
        embT = sb("embT", [128, FC, TB])
        xs = sb("xs", [128, (L + 1) * XC])
        x_bd = sb("x_bd", [128, 2, UP, KR])
        yv = sb("yv", [128, 2, UP, HF + D])
        v_sb = sb("v_sb", [128, SL, UP, D])
        s_sb = sb("s_sb", [KR, 2, UP, HF])
        p_sb = sb("p_sb", [KR, 2, UP, H, F])
        mx = sb("mx", [HF, 2 * UP])
        mhl = sb("mhl", [40, HF], F32R)
        rden = sb("rden", [128, C])
        att = sb("att", [128, C])
        pre = sb("pre", [128, SL, C])
        prod = sb("prod", [128, NP, F])
        red = sb("red", [128, TILES * NP])
        h1 = sb("h1", [128, N1])
        h1T = sb("h1T", [128, KC, 128])
        h2 = sb("h2", [128, N2])
        h2w = sb("h2w", [128, N2])
        dnn = sb("dnn", [128, TILES])
        att_o = sb("att_o", [128, TILES])
        dnn_o = sb("dnn_o", [128, TILES])
        tot = sb("tot", [128, TILES])
        y_out = sb("y_out", [TILES, 128])
        Yb, Tb, Ob, Hb = (bank(n) for n in ("Yb", "Tb", "Ob", "Hb"))
        SV = [ctx.enter_context(nc.psum_tensor(n, [128, 2 * W], F32)) for n in ("SV0", "SV1")]
        PW = HF + D
        TRB = [Tb, Yb, SV[0]]

        def sv_view(slot, rows, lo, hi):
            return SV[slot][rows, :].rearrange("q (b w) -> q b w", w=W)[:, :, 0:2 * PW].rearrange(
                "q b (p c) -> q b p c", c=PW)[:, :, :, lo:hi]

        def sv_at(slot, p, rows, lo, hi):
            at = (p // 2) * W + (p % 2) * PW
            return SV[slot][rows, at + lo:at + hi]

        ld_w = sem("ld_w")
        ld_i = sem("ld_i")
        ld_d = sem("ld_d")
        pre_pool = sem("pre_pool")
        pre_dve = sem("pre_dve")
        pre_pe = sem("pre_pe")
        weights_ready = sem("weights_ready")
        idx_ready = sem("idx_ready")
        gathered = sem("gathered")
        tr_ps = sem("tr_ps")
        embT_ready = sem("embT_ready")
        l1_ps = sem("l1_ps")
        h1_ready = sem("h1_ready")
        h1T_ps = sem("h1T_ps")
        h1T_ready = sem("h1T_ready")
        l2_ps = sem("l2_ps")
        x0_ready = sem("x0_ready")
        h_free = sem("h_free")
        lin_free = sem("lin_free")
        idx_copied = sem("idx_copied")
        red_done = sem("red_done")
        dchain = sem("dchain")
        pe_passed = sem("pe_passed")
        pool_passed = sem("pool_passed")
        x_copied = sem("x_copied")
        w_ready = sem("w_ready")
        y_ps = sem("y_ps")
        y_ready = sem("y_ready")
        s_ps = sem("s_ps")
        s_ready = sem("s_ready")
        t_ps = sem("t_ps")
        m_ready = sem("m_ready")
        mt_ps = sem("mt_ps")
        hi_ready = sem("hi_ready")
        mhl_ready = sem("mhl_ready")
        e_ps = sem("e_ps")
        den_ps = sem("den_ps")
        p_ready = sem("p_ready")
        o_ps = sem("o_ps")
        rden_ready = sem("rden_ready")
        att_ready = sem("att_ready")
        pre_ready = sem("pre_ready")
        x_new = sem("x_new")
        fin_pe = sem("fin_pe")
        fin_dve = sem("fin_dve")
        fin_act = sem("fin_act")
        stored = sem("stored")

        LD_W = 16 * (2 + 2 * L + 2 * L + 2)
        LD_D = 16 * 7

        block = ctx.enter_context(nc.Block())

        def each_group(eng, tile, step, last):
            for s in range(SL):
                step(tile, 0, s, 0)
            with eng.Fori(1, GROUPS) as g:
                for s in range(SL):
                    step(tile, g, s, 1)
            for s in range(SL):
                step(tile, None, s, 2)
                last(s)

        def w_count(tile, g, k):
            return (tile * GROUPS + g) * 2 + k

        def has(part, s, k):
            return (part == 0 and s - k >= 0) or part == 1 or (part == 2 and s - k < 0)

        def count(tile, g, part, s, k):
            return tile * NU + (NU if part == 2 else g * SL) + s - k + 1

        @block.sync
        def _(sp):
            sp.dma_start(idx_in[:], X.rearrange("(t p) f -> p t f", p=TB)).then_inc(ld_i, 16)
            sp.dma_start(w_in[:, 0:L, :], WQ.rearrange("l d c -> d l c")).then_inc(ld_w, 16)
            sp.dma_start(w_in[:, L:2 * L, :], WK.rearrange("l d c -> d l c")).then_inc(ld_w, 16)
            sp.wait_ge(pre_pool, 1)
            for l in range(L):
                for e in range(2):
                    lo = 64 * e
                    sp.dma_start(w_all[lo:lo + D, l, 256 + lo:256 + lo + D], WR[l]).then_inc(ld_w, 16)
                    sp.dma_start(w_all[lo:lo + D, l, 384:384 + D], WV[l]).then_inc(ld_w, 16)
            for e in range(2):
                sp.dma_start(wl_in[:, e, :], Wlin.rearrange("(f d) o -> f (d o)", f=F)).then_inc(ld_w, 16)
            sp.dma_start(w1[:, 0:FC - 1, :],
                         W1[0:(FC - 1) * 128, :].rearrange("(c p) n -> p c n", p=128)).then_inc(ld_d, 16)
            sp.dma_start(w1[0:LASTW, FC - 1, :], W1[(FC - 1) * 128:, :]).then_inc(ld_d, 16)
            sp.dma_start(w2[:], W2.rearrange("(c p) n -> p c n", p=128)).then_inc(ld_d, 16)
            sp.dma_start(b1_b[:], b1[None, :].to_broadcast([128, N1])).then_inc(ld_d, 16)
            sp.dma_start(b2_b[:], b2[None, :].to_broadcast([128, N2])).then_inc(ld_d, 16)
            sp.dma_start(w3_b[:], W3.rearrange("n o -> o n").to_broadcast([128, N2])).then_inc(ld_d, 16)
            sp.dma_start(b3_b[:], b3[None, :].to_broadcast([128, 1])).then_inc(ld_d, 16)
            sp.wait_ge(fin_act, 1)
            sp.dma_start(out.rearrange("(t p) o -> t (p o)", p=128), y_out[:]).then_inc(stored, 16)
            sp.wait_ge(stored, 16)

        @block.gpsimd
        def _(pool):
            nc.gpsimd.memset(w_all[:], 0.0).then_inc(pre_pool, 1)
            nc.gpsimd.iota(f_off[:], pattern=[[VOCAB, F]], base=0, channel_multiplier=0).then_inc(pre_pool, 1)
            nc.gpsimd.memset(ident[:], 0.0).then_inc(pre_pool, 1)
            nc.gpsimd.memset(sel_f[:], 0.0).then_inc(pre_pool, 1)
            pool.wait_ge(pre_pool, 4)
            nc.gpsimd.affine_select(out=ident[:], in_=ident[:], compare_op=ALU.not_equal, fill=1.0, base=0,
                                    pattern=[[-1, 128]], channel_multiplier=1).then_inc(pre_pool, 1)
            for part, row0 in enumerate((0, 32)):
                for e in range(2):
                    cols = sel_f[:, :, 64 * e:64 * e + F]
                    done = nc.gpsimd.affine_select(out=cols, in_=cols, compare_op=ALU.not_equal, fill=-1.0, base=-row0 - e,
                                                   pattern=[[-2, UP], [0, F]], channel_multiplier=1)
                done.then_inc(pre_pool, 1)
                if part == 0:
                    pool.wait_ge(pre_pool, 6)

            def gather():
                for f in range(F):
                    nc.gpsimd.indirect_dma_start(
                        out=emb[:, f * D:(f + 1) * D], out_offset=None, in_=table,
                        in_offset=bass.IndirectOffsetOnAxis(ap=idx_t[:, f:f + 1], axis=0),
                    ).then_inc(gathered, 16)

            pool.wait_ge(idx_ready, 1)
            nc.gpsimd.tensor_copy(idx_t[:], idx[:, 0:F]).then_inc(idx_copied, 1)
            pool.wait_ge(idx_copied, 1)
            gather()

            def lin(tile):
                pool.wait_ge(x_new, tile * NU + NU)
                nc.gpsimd.tensor_tensor(prod[:], xs[:, L * XC:(L + 1) * XC].rearrange("p (n f) -> p n f", f=F),
                                        wl[:, None, :].to_broadcast([128, NP, F]), ALU.mult).then_inc(lin_free, 1)

            with pool.Fori(0, TILES - 1) as tile:
                pool.wait_ge(tr_ps, (tile + 1) * NB)
                nc.gpsimd.tensor_copy(idx_t[:], idx[:, bass.ds((tile + 1) * F, F)]).then_inc(idx_copied, 1)
                pool.wait_ge(idx_copied, tile + 2)
                pool.sem_inc(pool_passed, 1)
                gather()
                lin(tile)
            lin(TILES - 1)

        @block.tensor
        def _(pe):
            pe.wait_ge(pre_pool, 5)
            pe.wait_ge(ld_w, LD_W)
            for k in range(2 * L):
                nc.tensor.transpose(Yb[0:D, k * D:(k + 1) * D], w_in[:, k, :], ident[0:D, 0:D])
            nc.tensor.transpose(Tb[0:128, 0:F], wl_in[:].rearrange("f e d -> f (e d)"),
                                ident[0:F, 0:F]).then_inc(pre_pe, 1)
            pe.wait_ge(pre_dve, 1)
            for l in range(L):
                for h in range(H):
                    for e in range(2):
                        last = nc.tensor.matmul([SV[1], SV[0]][h][64 * e:64 * e + D, l * D:(l + 1) * D],
                                                wT[DH * h:DH * (h + 1), l, :],
                                                wT[DH * h:DH * (h + 1), L + l, :], start=True, stop=True)
            last.then_inc(pre_pe, 1)

            def embed(tile):
                pe.wait_ge(h_free, tile + 1)
                pe.wait_ge(gathered, (tile + 1) * (16 * F))
                for k in range(NB):
                    if k >= 3:
                        pe.wait_ge(embT_ready, tile * NB + (k - 2))
                    for c in range(BK):
                        n = k * BK + c
                        w = LASTW if n == FC - 1 else 128
                        last = nc.tensor.transpose(TRB[k % 3][0:w, c * 128:(c + 1) * 128],
                                                   emb[:, n * 128:n * 128 + w], ident[:])
                    last.then_inc(tr_ps, 1)
                pe.wait_ge(embT_ready, (tile + 1) * NB)
                for n in range(FC):
                    w = LASTW if n == FC - 1 else 128
                    last = nc.tensor.matmul(Hb[:], embT[0:w, n, :], w1[0:w, n, :], start=(n == 0), stop=(n == FC - 1))
                last.then_inc(l1_ps, 1)

            def step(tile, g, s, part):
                def cnt(k):
                    return count(tile, g, part, s, k)

                if has(part, s, 3):
                    pe.wait_ge(p_ready, cnt(3))
                    pe.sem_inc(pe_passed, 1)
                elif has(part, s, 1):
                    pe.wait_ge(y_ready, cnt(1))
                    pe.sem_inc(pe_passed, 1)
                if has(part, s, 2):
                    pe.wait_ge(m_ready, cnt(2))
                    nc.tensor.transpose(Yb[0:2 * UP, 2 * C:2 * C + HF], mx[:], ident[0:HF, 0:HF]).then_inc(mt_ps, 1)
                if has(part, s, 1):
                    pe.wait_ge(x_copied, cnt(1))
                    for p in range(UP):
                        last = nc.tensor.matmul(sv_at((s - 1) % 2, p, slice(0, KR), 0, PW),
                                                x_bd[:, (s - 1) % 2, p, :], yv[:, (s - 1) % 2, p, :],
                                                start=(p % 2 == 0), stop=(p % 2 == 1), skip_group_check=True)
                    last.then_inc(s_ps, 1)
                if has(part, s, 2):
                    pe.wait_ge(mhl_ready, cnt(2))
                    pe.sem_inc(pe_passed, 1)
                if has(part, s, 0):
                    if s == 0:
                        pe.wait_ge(w_ready, w_count(tile, g, 1))
                    for h in range(H):
                        last = nc.tensor.matmul(Yb[:, h * C:(h + 1) * C], w_y[:, h * 128:(h + 1) * 128],
                                                xs[:, bass.ds((g * SL + s) * C, C)], start=True, stop=True)
                    last.then_inc(y_ps, 1)
                if has(part, s, 2):
                    for p in range(UP):
                        last = nc.tensor.matmul(sv_at(s % 2, p, slice(0, KR), 0, HF), sel[:, p * KR:(p + 1) * KR],
                                                mhl[:], start=False, stop=True, skip_group_check=True)
                    last.then_inc(e_ps, 1)
                if has(part, s, 1):
                    pe.wait_ge(s_ready, cnt(1))
                    for p in range(UP):
                        last = nc.tensor.transpose(Tb[0:HF, p * 128:p * 128 + KR], s_sb[:, (s - 1) % 2, p, :],
                                                   ident[0:KR, 0:KR])
                    last.then_inc(t_ps, 1)
                if has(part, s, 3):
                    if part == 1 or has(part, s, 4):
                        pe.wait_ge(pre_ready, cnt(4))
                    if part == 1 and s < 3:
                        at = (g * SL + (s - 3)) * C
                    else:
                        at = ((NU if part == 2 else g * SL) + s - 3) * C
                    if s == 3 and part < 2:
                        pe.wait_ge(w_ready, w_count(tile, g, 2))
                    for e in range(2):
                        for h in range(H):
                            po = 64 * e + DH * h
                            last = nc.tensor.matmul(Hb[po:po + DH, 0:C], ones[0:KR, e, :], p_sb[:, (s - 3) % 2, :, h, :],
                                                    start=True, stop=True)
                    last.then_inc(den_ps, 1)
                    nc.tensor.matmul(Ob[:, C:2 * C], w_r[:], xs[:, bass.ds(at, C)], start=True, stop=True)
                    for p in range(UP):
                        for e in range(2):
                            for h in range(H):
                                lo, po = 64 * e, 64 * e + DH * h
                                last = nc.tensor.matmul(Ob[po:po + DH, p * F:(p + 1) * F],
                                                        v_sb[lo:lo + F, (s - 3) % SL, p, DH * h:DH * (h + 1)],
                                                        p_sb[lo:lo + F, (s - 3) % 2, p, h, :],
                                                        start=True, stop=True)
                    last.then_inc(o_ps, 1)

            def tile_body(tile):
                embed(tile)
                pe.wait_ge(x0_ready, tile + 1)
                pe.sem_inc(pe_passed, 1)

                def last(s):
                    if s == 1:
                        pe.wait_ge(h1_ready, tile + 1)
                        for k in range(KC):
                            t = nc.tensor.transpose(Yb[:, k * 128:(k + 1) * 128], h1[:, k * 128:(k + 1) * 128], ident[:])
                        t.then_inc(h1T_ps, 1)
                    if s == 2:
                        pe.wait_ge(h1T_ready, tile + 1)
                        for k in range(KC):
                            t = nc.tensor.matmul(Tb[:, 0:N2], h1T[:, k, :], w2[:, k, :], start=(k == 0), stop=(k == KC - 1))
                        t.then_inc(l2_ps, 1)

                each_group(pe, tile, step, last)

            pe.wait_ge(weights_ready, 1)
            pe.wait_ge(ld_d, LD_D)
            with pe.Fori(0, TILES) as tile:
                tile_body(tile)
            pe.wait_ge(red_done, TILES)
            for t in range(TILES):
                for e in range(2):
                    lo = 64 * e
                    last = nc.tensor.matmul(Yb[lo:lo + NP, t:t + 1], red[lo:lo + D, t * NP:(t + 1) * NP],
                                            ones_c[lo:lo + D, :], start=True, stop=True)
            last.then_inc(fin_pe, 1)
            pe.wait_ge(fin_dve, 2)
            nc.tensor.transpose(Tb[0:TILES, 0:128], tot[:], ident[:]).then_inc(fin_pe, 1)

        @block.scalar
        def _(act):
            def step(tile, g, s, part):
                def cnt(k):
                    return count(tile, g, part, s, k)

                if has(part, s, 1):
                    act.wait_ge(s_ps, cnt(1))
                    nc.scalar.copy(s_sb[:, (s - 1) % 2, :, :].rearrange("q (b p) c -> q b p c", p=2),
                                   sv_view((s - 1) % 2, slice(0, KR), 0, HF)).then_inc(s_ready, 1)
                    nc.scalar.copy(v_sb[0:KR, (s - 1) % SL, :, :].rearrange("q (b p) c -> q b p c", p=2),
                                   sv_view((s - 1) % 2, slice(0, KR), HF, PW))
                if has(part, s, 0):
                    act.wait_ge(y_ps, cnt(0))
                    nc.scalar.copy(yv[:, s % 2, :, 0:HF].rearrange("q p (h f) -> q h p f", h=H),
                                   Yb[:, 0:H * C].rearrange("q (h p f) -> q h p f", h=H, p=UP)).then_inc(y_ready, 1)
                if has(part, s, 2):
                    act.wait_ge(e_ps, cnt(2))
                    nc.scalar.activation(p_sb[:, s % 2, :, :, :].rearrange("q (b p) h f -> q b p (h f)", p=2),
                                         sv_view(s % 2, slice(0, KR), 0, HF), ACTF.Exp).then_inc(p_ready, 1)
                if has(part, s, 4):
                    act.wait_ge(pre_ready, cnt(4))
                    if part == 1:
                        at = (g * SL + (s - 4 + UL)) * C
                    else:
                        at = ((NU if part == 2 else 0) + s - 4 + UL) * C
                    nc.scalar.activation(xs[:, bass.ds(at, C)], pre[:, s, :], ACTF.Relu).then_inc(x_new, 1)

            with act.Fori(0, TILES) as tile:
                for k in range(NB):
                    act.wait_ge(tr_ps, tile * NB + (k + 1))
                    src = TRB[k % 3]
                    if k == NB - 1:
                        n = BK - 1
                        nc.scalar.copy(embT[:, k * BK:k * BK + n, :].rearrange("q c b -> q (c b)"), src[:, 0:n * 128])
                        nc.scalar.copy(embT[0:LASTW, k * BK + n, :], src[0:LASTW, n * 128:W]).then_inc(embT_ready, 1)
                    else:
                        nc.scalar.copy(embT[:, k * BK:(k + 1) * BK, :].rearrange("q c b -> q (c b)"),
                                       src[:, 0:W]).then_inc(embT_ready, 1)
                act.wait_ge(lin_free, tile + 1)

                def last(s):
                    if s == 1:
                        act.wait_ge(h1T_ps, tile + 1)
                        nc.scalar.activation(h1T[:].rearrange("q k b -> q (k b)"), Yb[:], ACTF.Relu).then_inc(h1T_ready, 1)

                each_group(act, tile, step, last)
            act.wait_ge(fin_pe, 2)
            nc.scalar.activation(y_out[:], Tb[0:TILES, 0:128], ACTF.Sigmoid).then_inc(fin_act, 1)

        @block.vector
        def _(dve):
            nc.vector.memset(x_bd[:], 0.0)
            nc.vector.memset(mhl[:].bitcast(F32), 0.0)
            nc.vector.memset(ones[:], 0.0).then_inc(h_free, 1)
            dve.wait_ge(h_free, 1)
            dve.wait_ge(ld_i, 16)
            dve.wait_ge(pre_pool, 7)
            nc.vector.tensor_tensor(idx[:].rearrange("q (t f) -> q t f", f=F), idx_in[:],
                                    f_off[:, None, :].to_broadcast([128, TILES, F]), ALU.add).then_inc(idx_ready, 1)
            nc.vector.memset(ones_c[:], 1.0)
            for e in range(2):
                nc.vector.memset(ones[64 * e:64 * e + 32, e, :], 1.0)
                nc.vector.memset(ones[64 * e + 32:64 * e + F, e, :], 1.0)
            nc.vector.tensor_copy(sel[:], sel_f[:].rearrange("q p j -> q (p j)")).then_inc(lin_free, 1)
            dve.wait_ge(pre_pe, 1)
            nc.vector.tensor_copy(wl[:], Tb[:, 0:F])
            nc.vector.tensor_copy(wT[:].rearrange("q k d -> q (k d)"), Yb[0:D, 0:2 * L * D]).then_inc(pre_dve, 1)
            dve.wait_ge(pre_pe, 2)
            for e in range(2):
                lo = 64 * e
                for h in range(H):
                    last = nc.vector.tensor_copy(
                        w_all[lo:lo + D, :, h * 128 + lo:h * 128 + lo + D],
                        [SV[1], SV[0]][h][lo:lo + D, 0:L * D].rearrange("q (l d) -> q l d", l=L))
            last.then_inc(dchain, 1)
            dve.wait_ge(dchain, 1)
            for l in range(L):
                n = GROUPS // L
                last = nc.vector.tensor_copy(w_grp[:, l * n:(l + 1) * n, :],
                                             w_all[:, l:l + 1, :].to_broadcast([128, n, 512]))
            last.then_inc(weights_ready, 1)
            dve.wait_ge(weights_ready, 1)
            dve.wait_ge(ld_d, LD_D)

            def step(tile, g, s, part):
                def cnt(k):
                    return count(tile, g, part, s, k)

                if has(part, s, 4):
                    dve.wait_ge(o_ps, cnt(4))
                if has(part, s, 2):
                    dve.wait_ge(mt_ps, cnt(2))
                    nc.vector.tensor_copy(mhl[0:2 * UP, :], Yb[0:2 * UP, 2 * C:2 * C + HF]).then_inc(hi_ready, 1)
                    dve.wait_ge(hi_ready, cnt(2))
                    nc.vector.tensor_tensor(mhl[32:32 + 2 * UP, :], Yb[0:2 * UP, 2 * C:2 * C + HF],
                                            mhl[0:2 * UP, :].bitcast(F32), ALU.subtract).then_inc(mhl_ready, 1)
                if part < 2 and s == 0:
                    nc.vector.tensor_copy(w_y[:], w_grp[:, bass.ds(g, 1), 0:256].rearrange(
                        "q g c -> q (g c)")).then_inc(w_ready, 1)
                if has(part, s, 4):
                    dve.wait_ge(rden_ready, cnt(4))
                    nc.vector.tensor_tensor(att[:], Ob[:, 0:C], rden[:], ALU.mult).then_inc(att_ready, 1)
                if part < 2:
                    if s == 3:
                        nc.vector.tensor_copy(w_r[:], w_grp[:, bass.ds(g, 1), 256:384].rearrange(
                            "q g c -> q (g c)")).then_inc(w_ready, 1)
                    if s < 2:
                        nc.vector.tensor_copy(yv[:, s, :, HF:HF + D],
                                              w_grp[:, bass.ds(g, 1), 384:384 + D].to_broadcast([128, UP, D]))
                if has(part, s, 4):
                    dve.wait_ge(att_ready, cnt(4))
                    nc.vector.tensor_tensor(pre[:, s, :], Ob[:, C:2 * C], att[:], ALU.add).then_inc(pre_ready, 1)
                if part < 2:
                    for e in range(2):
                        lo = 64 * e
                        done = nc.vector.tensor_copy(x_bd[lo:lo + D, s % 2, :, lo:lo + F],
                                                     xs[lo:lo + D, bass.ds((g * SL + s) * C, C)].rearrange("q (p f) -> q p f", p=UP))
                    done.then_inc(x_copied, 1)
                if has(part, s, 1):
                    dve.wait_ge(t_ps, cnt(1))
                    nc.vector.tensor_reduce(mx[:], Tb[0:HF, :].rearrange("q (n j) -> q n j", j=64)[:, :, 0:F],
                                            AX.X, ALU.max).then_inc(m_ready, 1)
                if has(part, s, 3):
                    dve.wait_ge(den_ps, cnt(3))
                    nc.vector.reciprocal(rden[:], Hb[:, 0:C]).then_inc(rden_ready, 1)

            with dve.Fori(0, TILES) as tile:
                for k in range(NB):
                    dve.wait_ge(embT_ready, tile * NB + (k + 1))
                    for e in range(2):
                        for odd in range(2):
                            n = BK - 1 if odd and k == NB - 1 else BK
                            src = embT[64 * odd:64 * odd + D, k * BK:k * BK + n, NP * e:NP * (e + 1)]
                            dst = xs[64 * e:64 * e + D, 0:XC].rearrange("q (p f) -> q f p", f=F)
                            f0 = 2 * BK * k + odd
                            last = nc.vector.tensor_copy(dst[:, f0:f0 + 2 * (n - 1) + 1:2, :], src)
                last.then_inc(x0_ready, 1)
                dve.wait_ge(x0_ready, tile + 1)
                dve.wait_ge(l1_ps, tile + 1)
                nc.vector.tensor_tensor(h1[:], Hb[:], b1_b[:], ALU.add).then_inc(h1_ready, 1)

                def last_steps(s):
                    if s == 2:
                        dve.wait_ge(l2_ps, tile + 1)
                        nc.vector.tensor_tensor(h2[:], Tb[:, 0:N2], b2_b[:], ALU.add).then_inc(h_free, 1)
                        dve.wait_ge(h_free, tile + 2)
                        nc.vector.scalar_tensor_tensor(out=h2w[:], in0=h2[:], scalar=0.0, in1=w3_b[:],
                                                       op0=ALU.max, op1=ALU.mult).then_inc(dchain, 1)
                        dve.wait_ge(dchain, tile * 2 + 2)
                        nc.vector.tensor_reduce(dnn[:, bass.ds(tile, 1)], h2w[:], AX.X, ALU.add).then_inc(dchain, 1)

                each_group(dve, tile, step, last_steps)
                dve.wait_ge(lin_free, tile + 2)
                nc.vector.tensor_reduce(red[:, bass.ds(tile * NP, NP)], prod[:], AX.X, ALU.add).then_inc(red_done, 1)
            dve.wait_ge(fin_pe, 1)
            nc.vector.tensor_scalar(att_o[:], Yb[:, 0:TILES], 0.0, None, ALU.max)
            nc.vector.tensor_scalar(dnn_o[:], dnn[:], b3_b[:, 0:1], 0.0, ALU.add, ALU.max).then_inc(fin_dve, 1)
            dve.wait_ge(fin_dve, 1)
            nc.vector.tensor_tensor(tot[:], att_o[:], dnn_o[:], ALU.add).then_inc(fin_dve, 1)


_INS = ["r_X", "L0_rec_emb_table", "L0_rec_WQ", "L0_rec_WK", "L0_rec_WV", "L0_rec_WR", "L0_rec_W1", "L0_rec_b1",
        "L0_rec_W2", "L0_rec_b2", "L0_rec_W3", "L0_rec_b3", "L0_rec_Wlin"]


def kernel(**inputs):
    import numpy as np
    import concourse.bacc as bacc
    from concourse.bass_utils import run_bass_kernel_spmd

    nc = bacc.Bacc("TRN2", target_bir_lowering=False, num_devices=1)
    arrays, args = {}, []
    for name in _INS:
        a = np.ascontiguousarray(inputs[name])
        arrays[name] = a
        args.append(nc.dram_tensor(name, a.shape, mybir.dt.from_np(a.dtype), kind="ExternalInput").ap())
    out = nc.dram_tensor("y", (inputs["r_X"].shape[0], 1), F32, kind="ExternalOutput").ap()
    autoint(nc, *args, out)
    r = run_bass_kernel_spmd(nc, [arrays], core_ids=[0])
    return r.results[0]["y"]
```

```python
from contextlib import ExitStack

import concourse.bass as bass
from concourse import mybir

F32 = mybir.dt.float32
F32R = mybir.dt.float32r
BF16 = mybir.dt.bfloat16
I32 = mybir.dt.int32
ALU = mybir.AluOpType
ACTF = mybir.ActivationFunctionType
AX = mybir.AxisListType


def autoint(nc, X, table, WQ, WK, WV, WR, W1, b1, W2, b2, W3, b3, Wlin, out):
    BATCH, F = X.shape
    VOCAB = table.shape[0] // F
    D = table.shape[1]
    L = WQ.shape[0]
    H = 2
    DH = D // H
    N1, N2 = W1.shape[1], W2.shape[1]
    TB = 128
    TILES = BATCH // TB
    NP = TB // 2
    UP = 4
    C = UP * F
    UL = NP // UP
    NU = L * UL
    SL = 8
    VS = 4
    GROUPS = NU // SL
    MID = GROUPS // 2
    XC = NP * F
    FC = (F + 1) // 2
    LASTW = (F - 2 * (FC - 1)) * D
    BK = 4
    NB = FC // BK
    HF = H * F
    FOLDS = (F - 1).bit_length()
    MR = 64 + 2 * UP
    KR = 64 + F
    W = 512
    KC = N1 // 128

    ctx = ExitStack()
    with ctx:
        def sb(name, shape, dt=F32):
            return ctx.enter_context(nc.sbuf_tensor(name, shape, dt))

        def bank(name):
            return ctx.enter_context(nc.psum_tensor(name, [128, W], F32))

        def sem(name):
            return ctx.enter_context(nc.semaphore(name))

        ident = sb("ident", [128, 128])
        ones = sb("ones", [128, 2, DH])
        ones_c = sb("ones_c", [128, 1])
        sel_f = sb("sel_f", [MR, UP, KR])
        sel = sb("sel", [MR, UP * KR], BF16)
        w_in = sb("w_in", [D, 2 * L, D])
        wT = sb("wT", [D, 2 * L, D])
        w_all = sb("w_all", [128, L, 4 * 128])
        w_hi = sb("w_hi", [128, GROUPS, 3 * 128], F32R)
        w_lo = sb("w_lo", [128, GROUPS, 3 * 128], F32R)
        w_v = sb("w_v", [128, GROUPS, D])
        w_y = sb("w_y", [128, 2, 2 * 128], F32R)
        w_r = sb("w_r", [128, 2, 128], F32R)
        w1 = sb("w1", [128, FC, N1])
        w2 = sb("w2", [128, KC, N2])
        b1_b = sb("b1_b", [128, N1])
        b2_b = sb("b2_b", [128, N2])
        w3_b = sb("w3_b", [128, N2])
        b3_b = sb("b3_b", [128, 1])
        wl_in = sb("wl_in", [F, 2, D])
        wl = sb("wl", [128, F])
        idx_in = sb("idx_in", [128, TILES, F], I32)
        f_off = sb("f_off", [128, F], I32)
        idx = sb("idx", [128, TILES * F], I32)
        idx_t = sb("idx_t", [128, F], I32)
        emb = sb("emb", [128, F * D])
        embT = sb("embT", [128, FC, TB])
        xs = sb("xs", [128, (L + 1) * XC])
        x_hi = sb("x_hi", [128, SL // 2, 2 * C], F32R)
        x_lo = sb("x_lo", [128, SL // 2, 2 * C], F32R)
        x_bd = sb("x_bd", [128, 2, UP, KR])
        yv = sb("yv", [128, VS, UP, HF + D])
        v_sb = sb("v_sb", [128, VS, UP, D])
        s_sb = sb("s_sb", [KR, 2, UP, HF])
        p_sb = sb("p_sb", [KR, 2, UP, H, F])
        mx = sb("mx", [HF, 2 * UP])
        m_parts = sb("m_parts", [MR, HF], BF16)
        m_rest = sb("m_rest", [2 * UP, HF])
        rden = sb("rden", [128, C])
        att = sb("att", [128, C])
        pre = sb("pre", [128, VS, C])
        prod = sb("prod", [128, NP, F])
        red = sb("red", [128, TILES * NP])
        h1 = sb("h1", [128, N1])
        h1T = sb("h1T", [128, KC, 128])
        h2 = sb("h2", [128, N2])
        h2w = sb("h2w", [128, N2])
        dnn = sb("dnn", [128, TILES])
        att_o = sb("att_o", [128, TILES])
        dnn_o = sb("dnn_o", [128, TILES])
        tot = sb("tot", [128, TILES])
        y_out = sb("y_out", [TILES, 128])
        Yb, Tb, Ob, Hb = (bank(n) for n in ("Yb", "Tb", "Ob", "Hb"))
        SV = [ctx.enter_context(nc.psum_tensor(n, [128, 2 * W], F32)) for n in ("SV0", "SV1")]
        PW = HF + D

        def sv_view(slot, rows, lo, hi):
            return SV[slot][rows, :].rearrange("q (b w) -> q b w", w=W)[:, :, 0:2 * PW].rearrange(
                "q b (p c) -> q b p c", c=PW)[:, :, :, lo:hi]

        def sv_at(slot, p, rows, lo, hi):
            at = (p // 2) * W + (p % 2) * PW
            return SV[slot][rows, at + lo:at + hi]

        ld_w = sem("ld_w")
        ld_i = sem("ld_i")
        ld_d = sem("ld_d")
        pre_pool = sem("pre_pool")
        pre_dve = sem("pre_dve")
        pre_pe = sem("pre_pe")
        weights_ready = sem("weights_ready")
        idx_ready = sem("idx_ready")
        gathered = sem("gathered")
        first_gathered = [sem(f"first_gathered{k}") for k in range(NB)]
        tr_ps = sem("tr_ps")
        embT_ready = sem("embT_ready")
        l1_ps = sem("l1_ps")
        h1_ready = sem("h1_ready")
        h1T_ps = sem("h1T_ps")
        h1T_ready = sem("h1T_ready")
        l2_ps = sem("l2_ps")
        shuffled = sem("shuffled")
        h2_ready = sem("h2_ready")
        h2w_ready = sem("h2w_ready")
        lin_free = sem("lin_free")
        idx_copied = sem("idx_copied")
        red_done = sem("red_done")
        red_last = sem("red_last")
        dchain = sem("dchain")
        pe_passed = sem("pe_passed")
        act_passed = sem("act_passed")
        pool_passed = sem("pool_passed")
        x_copied = sem("x_copied")
        xh_ready = sem("xh_ready")
        xl_ready = sem("xl_ready")
        w_ready = sem("w_ready")
        y_ps = sem("y_ps")
        y_ready = sem("y_ready")
        s_ps = sem("s_ps")
        s_ready = sem("s_ready")
        t_ps = sem("t_ps")
        m_ready = sem("m_ready")
        mt_ps = sem("mt_ps")
        split = sem("split")
        m_split = sem("m_split")
        e_ps = sem("e_ps")
        den_ps = sem("den_ps")
        p_ready = sem("p_ready")
        o_ps = sem("o_ps")
        rden_ready = sem("rden_ready")
        att_ready = sem("att_ready")
        pre_ready = sem("pre_ready")
        x_new = sem("x_new")
        fin_pe = sem("fin_pe")
        fin_dve = sem("fin_dve")
        fin_act = sem("fin_act")
        stored = sem("stored")

        LD_W = 16 * (2 + 2 * L + 2 * L + 2)
        LD_D = 16 * 7

        block = ctx.enter_context(nc.Block())

        def walk(eng, step, middle=None):
            def rest(tile, inner):
                if middle is None:
                    with eng.Fori(1, GROUPS - 1) as g:
                        for s in range(SL):
                            step(tile * GROUPS + g, g, s, 1, None, tile)
                else:
                    with eng.Fori(1, MID) as g:
                        for s in range(SL):
                            step(tile * GROUPS + g, g, s, 1, None, tile)
                    middle(tile)
                    with eng.Fori(MID, GROUPS - 1) as g:
                        for s in range(SL):
                            step(tile * GROUPS + g, g, s, 1, None, tile)
                for s in range(SL):
                    step(tile * GROUPS + (GROUPS - 1), GROUPS - 1, s, 1, s if inner else None, tile)

            for s in range(SL):
                step(0, 0, s, 0, None, 0)
            with eng.Fori(0, TILES - 1) as tile:
                rest(tile, True)
                for s in range(SL):
                    step((tile + 1) * GROUPS, 0, s, 1, None, tile + 1)
            rest(TILES - 1, False)
            for s in range(SL):
                step(TILES * GROUPS, 0, s, 2, None, None)

        def unit_at(g, s, k):
            return NU + s - k if type(g) is int and g == 0 and s < k else g * SL + (s - k)

        def w_count(group, k):
            return group * 2 + k

        def next_two(group, g, s, extra):
            two, done = s // 2 + 1, group * (SL // 2) + (s // 2 + 2)
            if s < SL - 2:
                return (g * SL + (s + 2)) * C, two, done
            if type(g) is int and g == GROUPS - 1:
                return None if extra is None else (0, 0, done)
            return (g * SL + SL) * C, 0, done

        def has(part, s, k):
            return (part == 0 and s - k >= 0) or part == 1 or (part == 2 and s - k < 0)

        def count(group, s, k):
            return group * SL + (s - k + 1)

        @block.sync
        def _(sp):
            sp.dma_start(idx_in[:], X.rearrange("(t p) f -> p t f", p=TB)).then_inc(ld_i, 16)
            sp.dma_start(w_in[:, 0:L, :], WQ.rearrange("l d c -> d l c")).then_inc(ld_w, 16)
            sp.dma_start(w_in[:, L:2 * L, :], WK.rearrange("l d c -> d l c")).then_inc(ld_w, 16)
            sp.wait_ge(pre_pool, 1)
            for l in range(L):
                for e in range(2):
                    lo = 64 * e
                    sp.dma_start(w_all[lo:lo + D, l, 256 + lo:256 + lo + D], WR[l]).then_inc(ld_w, 16)
                    sp.dma_start(w_all[lo:lo + D, l, 384:384 + D], WV[l]).then_inc(ld_w, 16)
            for e in range(2):
                sp.dma_start(wl_in[:, e, :], Wlin.rearrange("(f d) o -> f (d o)", f=F)).then_inc(ld_w, 16)
            sp.dma_start(w1[:, 0:FC - 1, :],
                         W1[0:(FC - 1) * 128, :].rearrange("(c p) n -> p c n", p=128)).then_inc(ld_d, 16)
            sp.dma_start(w1[0:LASTW, FC - 1, :], W1[(FC - 1) * 128:, :]).then_inc(ld_d, 16)
            sp.dma_start(w2[:], W2.rearrange("(c p) n -> p c n", p=128)).then_inc(ld_d, 16)
            sp.dma_start(b1_b[:], b1[None, :].to_broadcast([128, N1])).then_inc(ld_d, 16)
            sp.dma_start(b2_b[:], b2[None, :].to_broadcast([128, N2])).then_inc(ld_d, 16)
            sp.dma_start(w3_b[:], W3.rearrange("n o -> o n").to_broadcast([128, N2])).then_inc(ld_d, 16)
            sp.dma_start(b3_b[:], b3[None, :].to_broadcast([128, 1])).then_inc(ld_d, 16)
            sp.wait_ge(fin_act, 1)
            sp.dma_start(out.rearrange("(t p) o -> t (p o)", p=128), y_out[:]).then_inc(stored, 16)
            sp.wait_ge(stored, 16)

        def shuffle_batch(eng, k, after=None):
            for e in range(2):
                for odd in range(2):
                    n = BK - 1 if odd and k == NB - 1 else BK
                    src = embT[64 * odd:64 * odd + D, k * BK:k * BK + n, NP * e:NP * (e + 1)]
                    dst = xs[64 * e:64 * e + D, 0:XC].rearrange("q (p f) -> q f p", f=F)
                    f0 = 2 * BK * k + odd
                    eng.tensor_copy(dst[:, f0:f0 + 2 * (n - 1) + 1:2, :], src).then_inc(shuffled, 1)
                    if after is not None:
                        after(k, e, odd)

        @block.gpsimd
        def _(pool):
            nc.gpsimd.memset(w_all[:], 0.0).then_inc(pre_pool, 1)
            nc.gpsimd.iota(f_off[:], pattern=[[VOCAB, F]], base=0, channel_multiplier=0).then_inc(pre_pool, 1)
            nc.gpsimd.memset(ident[:], 0.0).then_inc(pre_pool, 1)
            nc.gpsimd.memset(sel_f[:], 0.0).then_inc(pre_pool, 1)
            pool.wait_ge(pre_pool, 4)
            nc.gpsimd.affine_select(out=ident[:], in_=ident[:], compare_op=ALU.not_equal, fill=1.0, base=0,
                                    pattern=[[-1, 128]], channel_multiplier=1).then_inc(pre_pool, 1)
            for part, row0 in enumerate((0, 32, 64)):
                for e in range(2):
                    cols = sel_f[:, :, 64 * e:64 * e + F]
                    done = nc.gpsimd.affine_select(out=cols, in_=cols, compare_op=ALU.not_equal, fill=-1.0, base=-row0 - e,
                                                   pattern=[[-2, UP], [0, F]], channel_multiplier=1)
                done.then_inc(pre_pool, 1)
                if part < 2:
                    pool.wait_ge(pre_pool, 6 + part)

            def gather(first=False):
                for f in range(F):
                    done = first_gathered[f // (2 * BK)] if first else gathered
                    nc.gpsimd.indirect_dma_start(
                        out=emb[:, f * D:(f + 1) * D], out_offset=None, in_=table,
                        in_offset=bass.IndirectOffsetOnAxis(ap=idx_t[:, f:f + 1], axis=0),
                    ).then_inc(done, 16)

            pool.wait_ge(idx_ready, 1)
            nc.gpsimd.tensor_copy(idx_t[:], idx[:, 0:F]).then_inc(idx_copied, 1)
            pool.wait_ge(idx_copied, 1)
            gather(first=True)

            def lin(tile):
                pool.wait_ge(x_new, tile * NU + NU)
                nc.gpsimd.tensor_tensor(prod[:], xs[:, L * XC:(L + 1) * XC].rearrange("p (n f) -> p n f", f=F),
                                        wl[:, None, :].to_broadcast([128, NP, F]), ALU.mult).then_inc(lin_free, 1)
                pool.wait_ge(lin_free, tile + 2)
                pool.sem_inc(pool_passed, 1)
                n, done = F, 0
                while n > 1:
                    half = (n + 1) // 2
                    dst = red[:, bass.ds(tile * NP, NP)] if n == 2 else prod[:, :, 0:n - half]
                    a, b = prod[:, :, 0:n - half], prod[:, :, half:n]
                    if n == 2:
                        a, b = a.rearrange("p n o -> p (n o)"), b.rearrange("p n o -> p (n o)")
                    nc.gpsimd.tensor_tensor(dst, a, b, ALU.add).then_inc(red_done, 1)
                    n, done = half, done + 1
                    pool.wait_ge(red_done, tile * FOLDS + done)
                    pool.sem_inc(pool_passed, 1)

            def shuffle(tile):
                for k in range(NB):
                    pool.wait_ge(embT_ready, tile * NB + (k + 1))
                    pool.sem_inc(pool_passed, 1)

                    def one_at_a_time(k, e, odd):
                        pool.wait_ge(shuffled, tile * (NB * 4) + (k * 4 + e * 2 + odd + 1))
                        pool.sem_inc(pool_passed, 1)

                    shuffle_batch(nc.gpsimd, k, one_at_a_time)

            def gather_for(tile):
                pool.wait_ge(tr_ps, tile * NB)
                pool.sem_inc(pool_passed, 1)
                nc.gpsimd.tensor_copy(idx_t[:], idx[:, bass.ds(tile * F, F)]).then_inc(idx_copied, 1)
                pool.wait_ge(idx_copied, tile + 1)
                pool.sem_inc(pool_passed, 1)
                gather()

            gather_for(1)
            with pool.Fori(0, TILES - 2) as tile:
                shuffle(tile + 1)
                gather_for(tile + 2)
                lin(tile)
            shuffle(TILES - 1)
            lin(TILES - 2)

        @block.tensor
        def _(pe):
            pe.wait_ge(pre_pool, 5)
            pe.wait_ge(ld_w, LD_W)
            for k in range(2 * L):
                nc.tensor.transpose(Yb[0:D, k * D:(k + 1) * D], w_in[:, k, :], ident[0:D, 0:D])
            nc.tensor.transpose(Tb[0:128, 0:F], wl_in[:].rearrange("f e d -> f (e d)"),
                                ident[0:F, 0:F]).then_inc(pre_pe, 1)
            pe.wait_ge(pre_dve, 1)
            for l in range(L):
                for h in range(H):
                    for e in range(2):
                        last = nc.tensor.matmul([SV[1], SV[0]][h][64 * e:64 * e + D, l * D:(l + 1) * D],
                                                wT[DH * h:DH * (h + 1), l, :],
                                                wT[DH * h:DH * (h + 1), L + l, :], start=True, stop=True)
            last.then_inc(pre_pe, 1)

            def first_layer(out_ps, begin, end):
                for n in range(begin, end):
                    w = LASTW if n == FC - 1 else 128
                    last = nc.tensor.matmul(out_ps[:], embT[0:w, n, :], w1[0:w, n, :], start=(n == 0), stop=(n == FC - 1))
                return last

            def extra_work(k, t):
                if k < NB:
                    if type(t) is int and t == 0:
                        pe.wait_ge(first_gathered[k], 16 * min(2 * BK, F - 2 * BK * k))
                    elif k == 0:
                        pe.wait_ge(gathered, t * (16 * F))
                    for c in range(BK):
                        n = k * BK + c
                        w = LASTW if n == FC - 1 else 128
                        last = nc.tensor.transpose(Tb[0:w, c * 128:(c + 1) * 128], emb[:, n * 128:n * 128 + w], ident[:])
                    last.then_inc(tr_ps, 1)
                elif k == NB:
                    first_layer(Tb, 0, FC).then_inc(l1_ps, 1)
                elif k == NB + 1:
                    for c in range(KC):
                        last = nc.tensor.transpose(Tb[:, c * 128:(c + 1) * 128], h1[:, c * 128:(c + 1) * 128], ident[:])
                    last.then_inc(h1T_ps, 1)
                elif k == NB + 2:
                    for c in range(KC):
                        last = nc.tensor.matmul(Tb[:, 0:N2], h1T[:, c, :], w2[:, c, :], start=(c == 0), stop=(c == KC - 1))
                    last.then_inc(l2_ps, 1)

            def extra_read(k, t):
                if k < NB:
                    pe.wait_ge(embT_ready, t * NB + (k + 1))
                elif k == NB:
                    pe.wait_ge(h1_ready, t + 1)
                elif k == NB + 1:
                    pe.wait_ge(h1T_ready, t + 1)
                else:
                    pe.wait_ge(h2_ready, t + 1)
                pe.sem_inc(pe_passed, 1)

            def product(out_ps, w, at, slot):
                nc.tensor.matmul(out_ps, w[:, 0, at:at + 128], x_lo[:, slot, :], start=True, stop=False)
                nc.tensor.matmul(out_ps, w[:, 1, at:at + 128], x_hi[:, slot, :], start=False, stop=False)
                return nc.tensor.matmul(out_ps, w[:, 0, at:at + 128], x_hi[:, slot, :], start=False, stop=True)

            def step(group, g, s, part, extra, tile):
                def cnt(k):
                    return count(group, s, k)

                if has(part, s, 4):
                    pe.wait_ge(p_ready, cnt(4))
                    pe.sem_inc(pe_passed, 1)
                elif has(part, s, 1):
                    pe.wait_ge(y_ready, cnt(1))
                    pe.sem_inc(pe_passed, 1)
                if has(part, s, 4):
                    if part == 1 or has(part, s, 5):
                        pe.wait_ge(rden_ready, cnt(5))
                    for e in range(2):
                        for h in range(H):
                            po = 64 * e + DH * h
                            last = nc.tensor.matmul(Hb[po:po + DH, 0:C], ones[0:KR, e, :], p_sb[:, (s - 4) % 2, :, h, :],
                                                    start=True, stop=True)
                    last.then_inc(den_ps, 1)
                if has(part, s, 3):
                    pe.wait_ge(m_ready, cnt(3))
                    nc.tensor.transpose(Hb[0:2 * UP, C:C + HF], mx[:], ident[0:HF, 0:HF]).then_inc(mt_ps, 1)
                if has(part, s, 2):
                    pe.wait_ge(x_copied, cnt(2))
                    for p in range(UP):
                        last = nc.tensor.matmul(sv_at(s % 2, p, slice(0, KR), 0, PW),
                                                x_bd[:, s % 2, p, :], yv[:, (s - 2) % VS, p, :],
                                                start=(p % 2 == 0), stop=(p % 2 == 1), skip_group_check=True)
                    last.then_inc(s_ps, 1)
                if extra is not None:
                    extra_work(extra, tile + 1)
                if has(part, s, 0):
                    if s == 0:
                        pe.wait_ge(w_ready, w_count(group, 1))
                        pe.sem_inc(pe_passed, 1)
                    if s % 2 == 0:
                        pe.wait_ge(xl_ready, group * (SL // 2) + (s // 2 + 1))
                    product(Yb[:, 0:2 * C], w_y, (s % 2) * 128, s // 2).then_inc(y_ps, 1)
                if has(part, s, 4):
                    if (part == 1 or has(part, s, 5)) and (s % 2 == 0 or not has(part, s, 3)):
                        pe.wait_ge(pre_ready, cnt(5))
                        if s % 2 == 1 or s == 4:
                            pe.sem_inc(pe_passed, 1)
                    if s % 2 == 0:
                        if s == 4:
                            pe.wait_ge(w_ready, w_count(group, 2))
                        product(Ob[:, C:3 * C], w_r, 0, ((s - 4) % SL) // 2)
                if has(part, s, 3):
                    pe.wait_ge(m_split, cnt(3))
                    for p in range(UP):
                        last = nc.tensor.matmul(sv_at((s - 3) % 2, p, slice(0, KR), 0, HF), sel[:, p * KR:(p + 1) * KR],
                                                m_parts[:], start=False, stop=True, skip_group_check=True)
                    last.then_inc(e_ps, 1)
                if extra is not None:
                    extra_read(extra, tile + 1)
                if has(part, s, 2):
                    pe.wait_ge(s_ready, cnt(2))
                    for p in range(UP):
                        last = nc.tensor.transpose(Tb[0:HF, p * 128:p * 128 + KR], s_sb[:, s % 2, p, :],
                                                   ident[0:KR, 0:KR])
                    last.then_inc(t_ps, 1)
                if has(part, s, 4):
                    for p in range(UP):
                        for e in range(2):
                            for h in range(H):
                                lo, po = 64 * e, 64 * e + DH * h
                                last = nc.tensor.matmul(Ob[po:po + DH, p * F:(p + 1) * F],
                                                        v_sb[lo:lo + F, (s - 4) % VS, p, DH * h:DH * (h + 1)],
                                                        p_sb[lo:lo + F, (s - 4) % 2, p, h, :],
                                                        start=True, stop=True)
                    last.then_inc(o_ps, 1)

            pe.wait_ge(weights_ready, 1)
            pe.wait_ge(ld_d, LD_D)
            for k in range(NB + 3):
                if k == NB:
                    last.then_inc(l1_ps, 1)
                else:
                    extra_work(k, 0)
                extra_read(k, 0)
                if k < NB:
                    last = first_layer(Hb, k * BK, (k + 1) * BK)
            walk(pe, step)
            pe.wait_ge(red_done, (TILES - 1) * FOLDS)
            pe.wait_ge(red_last, 1)
            for t in range(TILES):
                for e in range(2):
                    lo = 64 * e
                    last = nc.tensor.matmul(Yb[lo:lo + NP, t:t + 1], red[lo:lo + D, t * NP:(t + 1) * NP],
                                            ones_c[lo:lo + D, :], start=True, stop=True)
            last.then_inc(fin_pe, 1)
            pe.wait_ge(fin_dve, 2)
            nc.tensor.transpose(Tb[0:TILES, 0:128], tot[:], ident[:]).then_inc(fin_pe, 1)

        @block.scalar
        def _(act):
            def extra_evac(k, t):
                if k < NB:
                    act.wait_ge(tr_ps, t * NB + (k + 1))
                    n = BK - 1 if k == NB - 1 else BK
                    last = nc.scalar.copy(embT[:, k * BK:k * BK + n, :].rearrange("q c b -> q (c b)"), Tb[:, 0:n * 128])
                    if n < BK:
                        last = nc.scalar.copy(embT[0:LASTW, k * BK + n, :], Tb[0:LASTW, n * 128:])
                    last.then_inc(embT_ready, 1)
                elif k == NB + 1:
                    act.wait_ge(h1T_ps, t + 1)
                    nc.scalar.activation(h1T[:].rearrange("q k b -> q (k b)"), Tb[:], ACTF.Relu).then_inc(h1T_ready, 1)

            def step(group, g, s, part, extra, tile):
                def cnt(k):
                    return count(group, s, k)

                if part < 2:
                    if s == 0:
                        for i, w in enumerate((w_hi, w_lo)):
                            done = nc.scalar.copy(w_y[:, i, :], w[:, bass.ds(g, 1), 0:256].rearrange("q g c -> q (g c)"))
                        done.then_inc(w_ready, 1)
                    if s == 3:
                        for i, w in enumerate((w_hi, w_lo)):
                            done = nc.scalar.copy(w_r[:, i, :], w[:, bass.ds(g, 1), 256:384].rearrange("q g c -> q (g c)"))
                        done.then_inc(w_ready, 1)
                    if s in (1, 3):
                        for slot in (s - 1, s):
                            nc.scalar.copy(yv[:, slot, :, HF:HF + D],
                                           w_v[:, bass.ds(g, 1), :].to_broadcast([128, UP, D]))
                if has(part, s, 1):
                    for e in range(2):
                        lo = 64 * e
                        done = nc.scalar.copy(x_bd[lo:lo + D, (s - 1) % 2, :, lo:lo + F],
                                              xs[lo:lo + D, bass.ds(unit_at(g, s, 1) * C, C)].rearrange("q (p f) -> q p f", p=UP))
                    done.then_inc(x_copied, 1)
                if part < 2 and s % 2 == 0:
                    two = next_two(group, g, s, extra)
                    if two is not None:
                        if s == SL - 2 and type(g) is int and g == GROUPS - 1:
                            act.wait_ge(shuffled, (tile + 2) * (NB * 4))
                            act.sem_inc(act_passed, 1)
                        nc.scalar.copy(x_hi[:, two[1], :], xs[:, bass.ds(two[0], 2 * C)]).then_inc(xh_ready, 1)
                if has(part, s, 2):
                    act.wait_ge(s_ps, cnt(2))
                    nc.scalar.copy(s_sb[:, s % 2, :, :].rearrange("q (b p) c -> q b p c", p=2),
                                   sv_view(s % 2, slice(0, KR), 0, HF)).then_inc(s_ready, 1)
                    nc.scalar.copy(v_sb[0:KR, (s - 2) % VS, :, :].rearrange("q (b p) c -> q b p c", p=2),
                                   sv_view(s % 2, slice(0, KR), HF, PW))
                if extra is not None:
                    extra_evac(extra, tile + 1)
                if has(part, s, 0):
                    act.wait_ge(y_ps, cnt(0))
                    h, u = s % 2, (s - s % 2) % VS
                    nc.scalar.copy(yv[:, u:u + 2, :, h * F:(h + 1) * F].rearrange("q u p f -> q (u p) f"),
                                   Yb[:, 0:2 * C].rearrange("q (n f) -> q n f", f=F)).then_inc(y_ready, 1)
                if has(part, s, 3):
                    act.wait_ge(e_ps, cnt(3))
                    nc.scalar.activation(p_sb[:, (s - 3) % 2, :, :, :].rearrange("q (b p) h f -> q b p (h f)", p=2),
                                         sv_view((s - 3) % 2, slice(0, KR), 0, HF), ACTF.Exp).then_inc(p_ready, 1)
                if has(part, s, 5):
                    act.wait_ge(pre_ready, cnt(5))
                    at = (unit_at(g, s, 5) + UL) * C
                    nc.scalar.activation(xs[:, bass.ds(at, C)], pre[:, s % VS, :], ACTF.Relu).then_inc(x_new, 1)

            def before_last_layer(tile):
                act.wait_ge(lin_free, tile + 1)
                act.sem_inc(act_passed, 1)

            act.wait_ge(weights_ready, 1)
            for k in range(NB + 3):
                extra_evac(k, 0)
            act.wait_ge(shuffled, NB * 4)
            nc.scalar.copy(x_hi[:, 0, :], xs[:, 0:2 * C]).then_inc(xh_ready, 1)
            walk(act, step, before_last_layer)
            act.wait_ge(fin_pe, 2)
            nc.scalar.activation(y_out[:], Tb[0:TILES, 0:128], ACTF.Sigmoid).then_inc(fin_act, 1)

        @block.vector
        def _(dve):
            nc.vector.memset(x_bd[:], 0.0)
            nc.vector.memset(m_parts[:], 0.0)
            nc.vector.memset(ones[:], 0.0).then_inc(dchain, 1)
            dve.wait_ge(dchain, 1)
            dve.wait_ge(ld_i, 16)
            dve.wait_ge(pre_pool, 8)
            nc.vector.tensor_tensor(idx[:].rearrange("q (t f) -> q t f", f=F), idx_in[:],
                                    f_off[:, None, :].to_broadcast([128, TILES, F]), ALU.add).then_inc(idx_ready, 1)
            nc.vector.memset(ones_c[:], 1.0)
            for e in range(2):
                nc.vector.memset(ones[64 * e:64 * e + 32, e, :], 1.0)
                nc.vector.memset(ones[64 * e + 32:64 * e + F, e, :], 1.0)
            nc.vector.tensor_copy(sel[:], sel_f[:].rearrange("q p j -> q (p j)")).then_inc(lin_free, 1)
            dve.wait_ge(pre_pe, 1)
            nc.vector.tensor_copy(wl[:], Tb[:, 0:F])
            nc.vector.tensor_copy(wT[:].rearrange("q k d -> q (k d)"), Yb[0:D, 0:2 * L * D]).then_inc(pre_dve, 1)
            dve.wait_ge(pre_pe, 2)
            for e in range(2):
                lo = 64 * e
                for h in range(H):
                    last = nc.vector.tensor_copy(
                        w_all[lo:lo + D, :, h * 128 + lo:h * 128 + lo + D],
                        [SV[1], SV[0]][h][lo:lo + D, 0:L * D].rearrange("q (l d) -> q l d", l=L))
            last.then_inc(dchain, 1)
            dve.wait_ge(dchain, 2)
            n = GROUPS // L
            for l in range(L):
                done = nc.vector.tensor_copy(w_v[:, l * n:(l + 1) * n, :],
                                             w_all[:, l:l + 1, 384:384 + D].to_broadcast([128, n, D]))
                done = nc.vector.tensor_copy(w_hi[:, l * n:(l + 1) * n, :],
                                             w_all[:, l:l + 1, 0:384].to_broadcast([128, n, 384]))
            done.then_inc(dchain, 1)
            dve.wait_ge(dchain, 3)
            for l in range(L):
                done = nc.vector.tensor_tensor(w_lo[:, l * n:(l + 1) * n, :],
                                               w_all[:, l:l + 1, 0:384].to_broadcast([128, n, 384]),
                                               w_hi[:, l * n:(l + 1) * n, :], ALU.subtract)
            done.then_inc(weights_ready, 1)
            dve.wait_ge(weights_ready, 1)
            dve.wait_ge(ld_d, LD_D)

            def extra_dnn(k, t, first_ps=Tb):
                if k == NB:
                    dve.wait_ge(l1_ps, t + 1)
                    nc.vector.tensor_tensor(h1[:], first_ps[:], b1_b[:], ALU.add).then_inc(h1_ready, 1)
                elif k == NB + 2:
                    dve.wait_ge(l2_ps, t + 1)
                    nc.vector.tensor_tensor(h2[:], Tb[:, 0:N2], b2_b[:], ALU.add).then_inc(h2_ready, 1)
                    dve.wait_ge(h2_ready, t + 1)
                    nc.vector.scalar_tensor_tensor(out=h2w[:], in0=h2[:], scalar=0.0, in1=w3_b[:],
                                                   op0=ALU.max, op1=ALU.mult).then_inc(h2w_ready, 1)
                    dve.wait_ge(h2w_ready, t + 1)
                    nc.vector.tensor_reduce(dnn[:, bass.ds(t, 1)], h2w[:], AX.X, ALU.add)

            def step(group, g, s, part, extra, tile):
                def cnt(k):
                    return count(group, s, k)

                m = Hb[0:2 * UP, C:C + HF]
                parts = [m_parts[32 * i:32 * i + 2 * UP, :] for i in range(3)]
                if has(part, s, 5):
                    dve.wait_ge(o_ps, cnt(5))
                    dve.wait_ge(rden_ready, cnt(5))
                    nc.vector.tensor_tensor(att[:], Ob[:, 0:C], rden[:], ALU.mult).then_inc(att_ready, 1)
                if has(part, s, 3):
                    dve.wait_ge(mt_ps, cnt(3))
                    nc.vector.tensor_copy(parts[0], m).then_inc(split, 1)
                if has(part, s, 5):
                    half = C + ((s - 5) % 2) * C
                    dve.wait_ge(att_ready, cnt(5))
                    nc.vector.tensor_tensor(pre[:, s % VS, :], Ob[:, half:half + C], att[:], ALU.add).then_inc(pre_ready, 1)
                if has(part, s, 3):
                    dve.wait_ge(split, cnt(3) * 3 - 2)
                    nc.vector.tensor_tensor(m_rest[:], m, parts[0], ALU.subtract).then_inc(split, 1)
                if has(part, s, 3):
                    dve.wait_ge(split, cnt(3) * 3 - 1)
                    nc.vector.tensor_copy(parts[1], m_rest[:]).then_inc(split, 1)
                    dve.wait_ge(split, cnt(3) * 3)
                    nc.vector.tensor_tensor(parts[2], m_rest[:], parts[1], ALU.subtract).then_inc(m_split, 1)
                if has(part, s, 4):
                    dve.wait_ge(den_ps, cnt(4))
                    nc.vector.reciprocal(rden[:], Hb[:, 0:C]).then_inc(rden_ready, 1)
                if extra is not None:
                    extra_dnn(extra, tile + 1)
                if has(part, s, 2):
                    dve.wait_ge(t_ps, cnt(2))
                    nc.vector.tensor_reduce(mx[:], Tb[0:HF, :].rearrange("q (n j) -> q n j", j=64)[:, :, 0:F],
                                            AX.X, ALU.max).then_inc(m_ready, 1)
                if part < 2 and s % 2 == 0:
                    two = next_two(group, g, s, extra)
                    if two is not None:
                        split_low(*two)

            def split_low(at, slot, done):
                dve.wait_ge(xh_ready, done)
                nc.vector.tensor_tensor(x_lo[:, slot, :], xs[:, bass.ds(at, 2 * C)], x_hi[:, slot, :],
                                        ALU.subtract).then_inc(xl_ready, 1)

            for k in range(NB):
                dve.wait_ge(embT_ready, k + 1)
                shuffle_batch(nc.vector, k)
            for k in range(NB, NB + 3):
                extra_dnn(k, 0, first_ps=Hb)
            split_low(0, 0, 1)
            walk(dve, step)
            dve.wait_ge(x_new, TILES * NU)
            dve.wait_ge(red_done, (TILES - 1) * FOLDS)
            nc.vector.tensor_tensor(prod[:], xs[:, L * XC:(L + 1) * XC].rearrange("p (n f) -> p n f", f=F),
                                    wl[:, None, :].to_broadcast([128, NP, F]), ALU.mult).then_inc(dchain, 1)
            dve.wait_ge(dchain, 4)
            nc.vector.tensor_reduce(red[:, (TILES - 1) * NP:], prod[:], AX.X, ALU.add).then_inc(red_last, 1)
            dve.wait_ge(fin_pe, 1)
            nc.vector.tensor_scalar(att_o[:], Yb[:, 0:TILES], 0.0, None, ALU.max)
            nc.vector.tensor_scalar(dnn_o[:], dnn[:], b3_b[:, 0:1], 0.0, ALU.add, ALU.max).then_inc(fin_dve, 1)
            dve.wait_ge(fin_dve, 1)
            nc.vector.tensor_tensor(tot[:], att_o[:], dnn_o[:], ALU.add).then_inc(fin_dve, 1)


_INS = ["r_X", "L0_rec_emb_table", "L0_rec_WQ", "L0_rec_WK", "L0_rec_WV", "L0_rec_WR", "L0_rec_W1", "L0_rec_b1",
        "L0_rec_W2", "L0_rec_b2", "L0_rec_W3", "L0_rec_b3", "L0_rec_Wlin"]


def kernel(**inputs):
    import numpy as np
    import concourse.bacc as bacc
    from concourse.bass_utils import run_bass_kernel_spmd

    nc = bacc.Bacc("TRN2", target_bir_lowering=False, num_devices=1)
    arrays, args = {}, []
    for name in _INS:
        a = np.ascontiguousarray(inputs[name])
        arrays[name] = a
        args.append(nc.dram_tensor(name, a.shape, mybir.dt.from_np(a.dtype), kind="ExternalInput").ap())
    out = nc.dram_tensor("y", (inputs["r_X"].shape[0], 1), F32, kind="ExternalOutput").ap()
    autoint(nc, *args, out)
    r = run_bass_kernel_spmd(nc, [arrays], core_ids=[0])
    return r.results[0]["y"]
```
